# Optimizing a Trainium2 kernel written in Bass

```python
import numpy as np
import jax
import jax.numpy as jnp

def _softmax(x, axis=-1):
    return jax.nn.softmax(x, axis=axis)

def _gelu(x):
    return jax.nn.gelu(x, approximate=True)

def _silu(x):
    return jax.nn.silu(x)

def _sigmoid(x):
    return jax.nn.sigmoid(x)

def _layernorm(x, axis=-1, eps=1e-05):
    m = jnp.mean(x, axis=axis, keepdims=True)
    v = jnp.var(x, axis=axis, keepdims=True)
    return (x - m) / jnp.sqrt(v + eps)

def _scatter_add(tgt, idx, src, axis=0):
    return tgt.at[idx].add(src)

def _segment_sum(src, seg, n):
    return jax.ops.segment_sum(src, seg, n)
kernel_name = 'mk_gnn_resnorm_d2_gnn_r32_a23627'

def setup_inputs(seed: int=0):
    np.random.seed(seed)
    _w = jnp.asarray

    def _rec_inputs():
        import jax
        import jax.numpy as jnp
        _gk = jax.random.key(seed)
        x = -0.0005121 + 1.001 * jax.random.normal(jax.random.fold_in(_gk, 1), (3125, 32), jnp.float32)
        src = jax.random.randint(jax.random.fold_in(_gk, 2), (100000,), 0, 3125, jnp.int32)
        dst = jnp.minimum((3125 * jax.random.uniform(jax.random.fold_in(_gk, 3), (100000,)) ** 2.0).astype(jnp.int32), 99999)
        _o = jnp.argsort(dst, stable=True)
        src = src[_o]
        dst = dst[_o]
        edge_attr_16 = -0.00019784 + 0.999804 * jax.random.normal(jax.random.fold_in(_gk, 12), (100000, 16), jnp.float32)
        return (x, src, dst, edge_attr_16)
    x, src, dst, edge_attr_16 = _rec_inputs()

    def _L0_gnn_setup():
        import jax, jax.numpy as jnp
        import numpy as np
        N_ATOMS = 3125
        N_EDGES = 12500
        ATOM_DIM = 32
        BOND_DIM = 16
        key = jax.random.key(seed)
        k1, k2, k3, k4 = jax.random.split(key, 4)
        atom_features = jax.random.normal(k1, (N_ATOMS, ATOM_DIM), dtype=jnp.float32)
        bond_features = jax.random.normal(k2, (N_EDGES, BOND_DIM), dtype=jnp.float32)
        pair_indices = jax.random.randint(k3, (N_EDGES, 2), 0, N_ATOMS, dtype=jnp.int64)
        limit = np.sqrt(6.0 / (BOND_DIM + ATOM_DIM * ATOM_DIM)).astype(np.float32)
        kernel = jax.random.uniform(k4, (BOND_DIM, ATOM_DIM * ATOM_DIM), dtype=jnp.float32, minval=-limit, maxval=limit)
        bias = jnp.zeros((ATOM_DIM * ATOM_DIM,), dtype=jnp.float32)
        return {'atom_features': atom_features, 'bond_features': bond_features, 'pair_indices': pair_indices, 'kernel': kernel, 'bias': bias}
    _L0_gnn_all = _L0_gnn_setup()
    _L0_gnn_in = {k: v for k, v in _L0_gnn_all.items() if k in ('kernel', 'bias')}
    del _L0_gnn_all

    def _L1_gnn_setup():
        import jax, jax.numpy as jnp
        import numpy as np
        N_NODES = 3125
        N_EDGES = 50000
        NODE_DIM = 32
        EDGE_DIM = 16
        OUT_DIM = 32
        key = jax.random.key(seed)
        ks = jax.random.split(key, 8)
        D = NODE_DIM + EDGE_DIM
        return {'y': jax.random.normal(ks[0], (N_NODES, NODE_DIM), dtype=jnp.float32), 'ex': jax.random.normal(ks[1], (N_EDGES, EDGE_DIM), dtype=jnp.float32), 'W1': jax.random.normal(ks[2], (D, D), dtype=jnp.float32) / np.sqrt(D), 'b1': jax.random.normal(ks[3], (D,), dtype=jnp.float32) * 0.01, 'W2': jax.random.normal(ks[4], (OUT_DIM, D), dtype=jnp.float32) / np.sqrt(D), 'b2': jax.random.normal(ks[5], (OUT_DIM,), dtype=jnp.float32) * 0.01, 'src': jax.random.randint(ks[6], (N_EDGES,), 0, N_NODES, dtype=jnp.int32), 'dst': jax.random.randint(ks[7], (N_EDGES,), 0, N_NODES, dtype=jnp.int32)}
    _L1_gnn_all = _L1_gnn_setup()
    _L1_gnn_in = {k: v for k, v in _L1_gnn_all.items() if k in ('W1', 'b1', 'W2', 'b2')}
    del _L1_gnn_all
    return {'x': x, 'src': src, 'dst': dst, 'edge_attr_16': edge_attr_16, 'L0_gnn_kernel': _L0_gnn_in['kernel'], 'L0_gnn_bias': _L0_gnn_in['bias'], 'L1_gnn_W1': _L1_gnn_in['W1'], 'L1_gnn_b1': _L1_gnn_in['b1'], 'L1_gnn_W2': _L1_gnn_in['W2'], 'L1_gnn_b2': _L1_gnn_in['b2']}

def reference(x, src, dst, edge_attr_16, L0_gnn_kernel, L0_gnn_bias, L1_gnn_W1, L1_gnn_b1, L1_gnn_W2, L1_gnn_b2):
    import jax
    import jax.numpy as jnp

    def _L0_gnn_ref(atom_features, bond_features, pair_indices, kernel, bias):
        import jax, jax.numpy as jnp
        import numpy as np
        N_ATOMS = 3125
        N_EDGES = 12500
        ATOM_DIM = 32
        BOND_DIM = 16
        n_atoms, d = atom_features.shape
        e = bond_features.shape[0]
        edge_mats = (bond_features @ kernel + bias).reshape(e, d, d)
        neighbors = atom_features[pair_indices[:, 1]]
        transformed = jnp.einsum('eij,ej->ei', edge_mats, neighbors)
        return jax.ops.segment_sum(transformed, pair_indices[:, 0], num_segments=n_atoms)

    def _L1_gnn_ref(y, ex, W1, b1, W2, b2, src, dst):
        import jax, jax.numpy as jnp
        import numpy as np
        N_NODES = 3125
        N_EDGES = 50000
        NODE_DIM = 32
        EDGE_DIM = 16
        OUT_DIM = 32
        n_nodes = y.shape[0]
        feat = jnp.concatenate([y[src], ex], axis=1)
        m = jax.nn.relu(feat @ W1.T + b1)
        s = jax.ops.segment_sum(m, dst, num_segments=n_nodes)
        cnt = jax.ops.segment_sum(jnp.ones((m.shape[0],), m.dtype), dst, num_segments=n_nodes)
        z = jnp.where(cnt[:, None] > 0, s / jnp.maximum(cnt, 1.0)[:, None], 0.0)
        h = jax.nn.relu(z @ W2.T + b2)
        return h
    edge_index_t = jnp.stack([src, dst], axis=1)
    x = _layernorm(x + _L0_gnn_ref(x, edge_attr_16, edge_index_t, L0_gnn_kernel, L0_gnn_bias), axis=-1)
    x = _layernorm(x + _L1_gnn_ref(x, edge_attr_16, L1_gnn_W1, L1_gnn_b1, L1_gnn_W2, L1_gnn_b2, src, dst), axis=-1)
    return x

_drawn_inputs = setup_inputs


def setup_inputs(seed=0):
    import zlib

    import numpy as np

    out = dict(_drawn_inputs(seed))
    spreads = {'L0_gnn_bias': (0.0, 0.1)}
    factors = {'L1_gnn_b1': 8.0, 'L1_gnn_b2': 7.444}
    for name, (base, spread) in spreads.items():
        noise = np.random.default_rng([zlib.crc32(name.encode()), seed]).standard_normal(out[name].shape)
        drawn = base * np.exp(spread * noise) if base else spread * noise
        out[name] = jnp.asarray(drawn.astype(out[name].dtype))
    for name, factor in factors.items():
        out[name] = (out[name] * factor).astype(out[name].dtype)
    return out
```

```python
from contextlib import ExitStack

import concourse.bass as bass
import numpy as np
from concourse import mybir

F32 = mybir.dt.float32
BF16 = mybir.dt.bfloat16
I16 = mybir.dt.int16
I32 = mybir.dt.int32
ALU = mybir.AluOpType
ACT = mybir.ActivationFunctionType
AX = mybir.AxisListType

EDGE_TILE = 125
GROUP_TILES = 4
GROUP = EDGE_TILE * GROUP_TILES
SUPER_GROUPS = 2
SUPER = GROUP * SUPER_GROUPS
NODE_TILE = 128
BANK = 512
PARTS = 3
WINDOW = 2
BATCH = 16
EPS = 1e-5


def wait(engine, semaphore, value):
    if not (isinstance(value, int) and value <= 0):
        engine.wait_ge(semaphore, value)


def paired_loop(engine, count, body):
    body(0, 0)
    body(1, 1)
    with engine.Fori(1, count // 2) as r:
        body(r * 2, 0)
        body(r * 2 + 1, 1)


def gnn_program(nc, x, src_rows, dst_rows, src_cols, dst_cols, bond_rows, edge_kernel, edge_bias, w1_node, w1_edge,
                b1, w2, b2, node_row, node_col, tile_starts, spread_bond, spread_x, sum_parts, out):
    N, D = x.shape
    E = src_rows.shape[0]
    BOND = bond_rows.shape[0]
    HID = w1_node.shape[1]
    TILES = E // EDGE_TILE
    GROUPS = E // GROUP
    SUPERS = E // SUPER
    BATCHES = TILES // BATCH
    NODE_TILES = -(-N // NODE_TILE)
    FULL = N // NODE_TILE
    TAIL = N - FULL * NODE_TILE
    NODES = NODE_TILES * NODE_TILE
    CHUNKS = BOND * D // 128
    COLS = PARTS * D + 1
    ACC_BANKS = -(-NODES // BANK)
    ROWS_DST, ROWS_DST_NEAR, ROWS_SRC = range(3)

    top = ExitStack()

    def sb(ctx, name, shape, dt):
        return ctx.enter_context(nc.sbuf_tensor(name, shape, dt))

    def pb(ctx, name, shape, dt=F32):
        return ctx.enter_context(nc.psum_tensor(name, shape, dt))

    def sem(name):
        return top.enter_context(nc.semaphore(name))

    row_table = nc.dram_tensor("row_table", (3, E), I16, kind="Internal").ap()
    bond_parts = nc.dram_tensor("bond_parts", (PARTS, BOND * E), BF16, kind="Internal").ap()
    first_tile_f_dram = nc.dram_tensor("first_tile_f_dram", (1, GROUPS), F32, kind="Internal").ap()
    first_tile_i_dram = nc.dram_tensor("first_tile_i_dram", (1, GROUPS), I32, kind="Internal").ap()
    spread_dram = nc.dram_tensor("spread_dram", (1, GROUPS), F32, kind="Internal").ap()

    node_feats = sb(top, "node_feats", [128, NODE_TILES, D], F32)
    node_parts = sb(top, "node_parts", [128, NODE_TILES, PARTS * D], BF16)
    node_iota = sb(top, "node_iota", [EDGE_TILE, NODES], I16)
    node_id = sb(top, "node_id", [128, NODE_TILES], F32)
    src_col = sb(top, "src_col", [EDGE_TILE, TILES], F32)
    dst_col = sb(top, "dst_col", [EDGE_TILE, TILES], F32)
    dst_near_col = sb(top, "dst_near_col", [EDGE_TILE, TILES], F32)
    first_tile = sb(top, "first_tile", [1, GROUPS], I32)
    is_near = sb(top, "is_near", [1, 1], I32)
    kernel_sb = sb(top, "kernel_sb", [128, CHUNKS, D], F32)
    bias_sb = sb(top, "bias_sb", [128, D], F32)
    w1_node_parts = sb(top, "w1_node_parts", [PARTS * D, PARTS, HID], BF16)
    w1_edge_parts = sb(top, "w1_edge_parts", [PARTS * BOND, PARTS, HID], BF16)
    b1_sb = sb(top, "b1_sb", [HID, 1], F32)
    w2_sb = sb(top, "w2_sb", [128, D], F32)
    b2_sb = sb(top, "b2_sb", [128, D], F32)
    spread_bond_sb = sb(top, "spread_bond_sb", [128, CHUNKS, 128], BF16)
    spread_x_sb = sb(top, "spread_x_sb", [PARTS * D, 128], BF16)
    sum_parts_sb = sb(top, "sum_parts_sb", [COLS, D + 1], F32)
    zeros = sb(top, "zeros", [128, BANK], BF16)

    def split(engine_step, vec, parts, whole, rest):
        engine_step(vec.tensor_copy(parts[0], whole))
        engine_step(vec.tensor_tensor(rest, whole, parts[0], ALU.subtract))
        engine_step(vec.tensor_copy(parts[1], rest))
        engine_step(vec.tensor_tensor(parts[2], rest, parts[1], ALU.subtract))

    with ExitStack() as ctx:
        PREP = GROUPS // 2
        PER = GROUPS // PREP
        PIECES = 4
        PIECE = BOND * E // (EDGE_TILE * PIECES)
        rows_i = sb(ctx, "rows_i", [PREP, PER * GROUP], I32)
        rows_f = sb(ctx, "rows_f", [PREP, PER * GROUP], F32)
        src_i = sb(ctx, "src_i", [PREP, PER * GROUP], I32)
        src_16 = sb(ctx, "src_16", [PREP, PER * GROUP], I16)
        dst_16 = sb(ctx, "dst_16", [PREP, PER * GROUP], I16)
        near_16 = sb(ctx, "near_16", [PREP, PER * GROUP], I16)
        low = sb(ctx, "low", [PREP, PER], F32)
        high = sb(ctx, "high", [PREP, PER], F32)
        low_tile = sb(ctx, "low_tile", [PREP, PER], F32)
        low_tile_i = sb(ctx, "low_tile_i", [PREP, PER], I32)
        high_tile = sb(ctx, "high_tile", [PREP, PER], F32)
        low_node = sb(ctx, "low_node", [PREP, PER], F32)
        spread = sb(ctx, "spread", [PREP, PER], F32)
        at_least = sb(ctx, "at_least", [PREP, NODE_TILES], F32)
        starts = sb(ctx, "starts", [PREP, NODE_TILES], F32)
        col_i = sb(ctx, "col_i", [EDGE_TILE, 2, TILES], I32)
        first_tile_f = sb(ctx, "first_tile_f", [EDGE_TILE, GROUPS], F32)
        spread_row = sb(ctx, "spread_row", [1, GROUPS], F32)
        widest = sb(ctx, "widest", [1, 1], F32)
        node_rest = sb(ctx, "node_rest", [128, NODE_TILES, D], F32)
        w_node_f = sb(ctx, "w_node_f", [PARTS * D, 2, HID], F32)
        w_edge_f = sb(ctx, "w_edge_f", [PARTS * BOND, 2, HID], F32)
        spread_bond_f = sb(ctx, "spread_bond_f", [PARTS * BOND, CHUNKS, 128], F32)
        spread_x_f = sb(ctx, "spread_x_f", [PARTS * D, 128], F32)
        bond_f = sb(ctx, "bond_f", [EDGE_TILE, 2, PIECE], F32)
        bond_rest = sb(ctx, "bond_rest", [EDGE_TILE, PIECE], F32)
        bond_p = sb(ctx, "bond_p", [EDGE_TILE, 2, PARTS, PIECE], BF16)

        cleared = sem("cleared")
        rows_loaded = sem("rows_loaded")
        cols_loaded = sem("cols_loaded")
        nodes_loaded = sem("nodes_loaded")
        consts_loaded = sem("consts_loaded")
        bond_loaded = [sem(f"bond_loaded{i}") for i in range(2)]
        bond_high = sem("bond_high")
        bond_rested = sem("bond_rested")
        bond_middle = sem("bond_middle")
        bond_low = sem("bond_low")
        bond_stored = [sem(f"bond_stored{i}") for i in range(2)]
        tiles_known = sem("tiles_known")
        rows_ready = sem("rows_ready")
        prep_stored = sem("prep_stored")
        rows_stored = sem("rows_stored")
        near_loaded = sem("near_loaded")
        prep_step = sem("prep_step")

        bond_view = bond_rows.rearrange("b e -> (b e)").rearrange("(p c) -> p c", p=EDGE_TILE)
        part_view = bond_parts.rearrange("s (p c) -> p s c", p=EDGE_TILE)
        by_prep = lambda row: row.rearrange("(q c) -> q c", q=PREP)

        with nc.Block() as block:
            @block.sync
            def _(sp):
                sp.dma_start(rows_i[:, :], by_prep(dst_rows)).then_inc(rows_loaded, 16)
                sp.dma_start(src_i[:, :], by_prep(src_rows)).then_inc(rows_loaded, 16)
                sp.dma_start(starts[:, :], tile_starts.partition_broadcast(PREP)).then_inc(rows_loaded, 16)
                for i in range(PIECES):
                    wait(sp, bond_rested, i - 1)
                    sp.dma_start(bond_f[:, i % 2, :], bond_view[:, i * PIECE:(i + 1) * PIECE]).then_inc(bond_loaded[i % 2], 16)
                    if i == 0:
                        sp.dma_start(col_i[:, 0, :], src_cols).then_inc(cols_loaded, 16)
                        sp.dma_start(col_i[:, 1, :], dst_cols).then_inc(cols_loaded, 16)
                        sp.wait_ge(cleared, 1)
                        sp.dma_start(node_feats[:, 0:FULL, :], x[0:FULL * NODE_TILE, :].rearrange("(h p) d -> p h d", p=NODE_TILE)).then_inc(nodes_loaded, 16)
                        sp.dma_start(node_feats[0:TAIL, FULL, :], x[FULL * NODE_TILE:N, :]).then_inc(nodes_loaded, 16)
                for i in range(PIECES):
                    sp.wait_ge(bond_low, i + 1)
                    sp.dma_start(part_view[:, :, i * PIECE:(i + 1) * PIECE], bond_p[:, i % 2, :, :]).then_inc(bond_stored[i % 2], 16)
                for i in range(2):
                    sp.wait_ge(bond_stored[i], 16 * (PIECES // 2))

            @block.gpsimd
            def _(pool):
                for t in (node_feats[:, FULL, :], bias_sb[:, :], w2_sb[:, :], spread_bond_sb[:, :, :]):
                    last = nc.gpsimd.memset(t, 0.0)
                last.then_inc(cleared, 1)
                nc.gpsimd.memset(zeros[:, :], 0.0)
                pool.wait_ge(cleared, 1)
                loads = [(node_iota[:, :], node_row.partition_broadcast(EDGE_TILE)), (node_id[:, :], node_col),
                         (kernel_sb[:, :, :], edge_kernel), (bias_sb[0:D, :], edge_bias), (b1_sb[:, :], b1),
                         (w2_sb[0:HID, :], w2), (b2_sb[:, :], b2.partition_broadcast(128)),
                         (spread_bond_f[:, :, :], spread_bond), (spread_x_f[:, :], spread_x),
                         (sum_parts_sb[:, :], sum_parts)]
                loads += [(w_node_f[i * D:(i + 1) * D, 0, :], w1_node) for i in range(PARTS)]
                loads += [(w_edge_f[i * BOND:(i + 1) * BOND, 0, :], w1_edge) for i in range(PARTS)]
                for to, of in loads:
                    pool.dma_start(to, of).then_inc(consts_loaded, 16)
                pool.wait_ge(consts_loaded, 16 * len(loads))

            @block.scalar
            def _(act):
                for i in range(PIECES):
                    act.wait_ge(bond_loaded[i % 2], 16 * (i // 2 + 1))
                    if i >= 2:
                        act.wait_ge(bond_stored[i % 2], 16 * (i // 2))
                    nc.scalar.activation(bond_p[:, i % 2, 0, :], bond_f[:, i % 2, :], ACT.Copy).then_inc(bond_high, 1)
                    act.wait_ge(bond_rested, i + 1)
                    nc.scalar.activation(bond_p[:, i % 2, 1, :], bond_rest[:, :], ACT.Copy).then_inc(bond_middle, 1)
                    if i == 1:
                        act.wait_ge(rows_ready, 1)
                        act.dma_start(by_prep(row_table[ROWS_DST, :]), dst_16[:, :]).then_inc(rows_stored, 16)
                        act.dma_start(by_prep(row_table[ROWS_DST_NEAR, :]), near_16[:, :]).then_inc(rows_stored, 16)
                        act.dma_start(by_prep(row_table[ROWS_SRC, :]), src_16[:, :]).then_inc(rows_stored, 16)
                        act.wait_ge(tiles_known, 1)
                        act.dma_start(first_tile_f_dram.rearrange("o (q c) -> (o q) c", q=PREP), low_tile[:, :]).then_inc(prep_stored, 16)
                        act.dma_start(first_tile_i_dram.rearrange("o (q c) -> (o q) c", q=PREP), low_tile_i[:, :]).then_inc(prep_stored, 16)
                        act.dma_start(spread_dram.rearrange("o (q c) -> (o q) c", q=PREP), spread[:, :]).then_inc(prep_stored, 16)
                        act.wait_ge(prep_stored, 48)
                        act.dma_start(first_tile_f[:, :], first_tile_f_dram.partition_broadcast(EDGE_TILE)).then_inc(near_loaded, 16)
                        act.dma_start(first_tile[:, :], first_tile_i_dram).then_inc(near_loaded, 16)
                        act.dma_start(spread_row[:, :], spread_dram).then_inc(near_loaded, 16)
                act.wait_ge(rows_stored, 48)

            @block.vector
            def _(dve):
                done = [0]

                def step(instruction):
                    done[0] += 1
                    instruction.then_inc(prep_step, 1)
                    dve.wait_ge(prep_step, done[0])

                v = nc.vector

                def bond_piece(i):
                    dve.wait_ge(bond_high, i + 1)
                    wait(dve, bond_middle, i)
                    step(v.tensor_tensor(bond_rest[:, :], bond_f[:, i % 2, :], bond_p[:, i % 2, 0, :], ALU.subtract))
                    v.sem_inc(bond_rested, 1)
                    dve.wait_ge(bond_middle, i + 1)
                    v.tensor_tensor(bond_p[:, i % 2, 2, :], bond_rest[:, :], bond_p[:, i % 2, 1, :], ALU.subtract).then_inc(bond_low, 1)
                    dve.wait_ge(bond_low, i + 1)

                dve.wait_ge(rows_loaded, 48)
                step(v.tensor_copy(rows_f[:, :], rows_i[:, :]))
                groups = rows_f[:, :].rearrange("q (g e) -> q g e", g=PER)
                step(v.tensor_reduce(low[:, :], groups, AX.X, ALU.min))
                step(v.tensor_reduce(high[:, :], groups, AX.X, ALU.max))
                for g in range(PER):
                    step(v.tensor_scalar(at_least[:, 1:NODE_TILES - 1], starts[:, 1:NODE_TILES - 1], low[:, g:g + 1], None,
                                         ALU.is_le, ALU.add, accum_out=low_tile[:, g:g + 1]))
                    step(v.tensor_scalar(at_least[:, 1:NODE_TILES], starts[:, 1:NODE_TILES], high[:, g:g + 1], None,
                                         ALU.is_le, ALU.add, accum_out=high_tile[:, g:g + 1]))
                step(v.tensor_tensor(spread[:, :], high_tile[:, :], low_tile[:, :], ALU.subtract))
                step(v.tensor_copy(low_tile_i[:, :], low_tile[:, :]))
                step(v.tensor_scalar(low_node[:, :], low_tile[:, :], float(NODE_TILE), None, ALU.mult))
                v.sem_inc(tiles_known, 1)
                step(v.tensor_copy(dst_16[:, :], rows_i[:, :]))
                for g in range(PER):
                    at = slice(g * GROUP, (g + 1) * GROUP)
                    step(v.tensor_scalar(near_16[:, at], rows_f[:, at], low_node[:, g:g + 1], None, ALU.subtract))
                step(v.tensor_copy(src_16[:, :], src_i[:, :]))
                v.sem_inc(rows_ready, 1)
                for i in range(PIECES):
                    bond_piece(i)
                dve.wait_ge(cols_loaded, 32)
                step(v.tensor_copy(src_col[:, :], col_i[:, 0, :]))
                step(v.tensor_copy(dst_col[:, :], col_i[:, 1, :]))
                dve.wait_ge(near_loaded, 48)
                step(v.tensor_scalar(first_tile_f[:, :], first_tile_f[:, :], float(NODE_TILE), None, ALU.mult))
                step(v.tensor_tensor(dst_near_col[:, :].rearrange("p (g t) -> p g t", g=GROUPS),
                                     dst_col[:, :].rearrange("p (g t) -> p g t", g=GROUPS),
                                     first_tile_f[:, :].unsqueeze(2).to_broadcast([EDGE_TILE, GROUPS, GROUP_TILES]), ALU.subtract))
                step(v.tensor_reduce(widest[:, :], spread_row[:, :], AX.X, ALU.max))
                step(v.tensor_scalar(is_near[:, :], widest[:, :], float(WINDOW - 1), None, ALU.is_le))
                dve.wait_ge(nodes_loaded, 32)
                split(step, v, [node_parts[:, :, i * D:(i + 1) * D] for i in range(PARTS)], node_feats[:, :, :], node_rest[:, :, :])
                dve.wait_ge(consts_loaded, 16 * 16)
                step(v.tensor_copy(spread_bond_sb[0:PARTS * BOND, :, :], spread_bond_f[:, :, :]))
                step(v.tensor_copy(spread_x_sb[:, :], spread_x_f[:, :]))
                split(step, v, [w1_node_parts[:, i, :] for i in range(PARTS)], w_node_f[:, 0, :], w_node_f[:, 1, :])
                split(step, v, [w1_edge_parts[:, i, :] for i in range(PARTS)], w_edge_f[:, 0, :], w_edge_f[:, 1, :])

    messages = sb(top, "messages", [EDGE_TILE, TILES, D], F32)
    bond_tile = bond_parts.rearrange("s (b e) -> (s b) e", b=BOND)

    def message_stage(layer):
        ctx = ExitStack()
        name = lambda n: f"{n}_m{layer}"
        index = sb(ctx, name("index"), [128, 2, SUPER], I16)
        bond = sb(ctx, name("bond"), [128, 2, SUPER], BF16)
        pick = sb(ctx, name("pick"), [128, 5, SUPER], BF16)
        gathered = sb(ctx, name("gathered"), [PARTS * D, 2, SUPER], BF16)
        gather_ps = pb(ctx, name("gather_ps"), [PARTS * D, SUPER_GROUPS, BANK])
        send_ps = pb(ctx, name("send_ps"), [EDGE_TILE, GROUP_TILES, D])

        index_loaded = [sem(name(f"index_loaded{i}")) for i in range(2)]
        bond_loaded = [sem(name(f"bond_loaded{i}")) for i in range(2)]
        bond_cleared = sem(name("bond_cleared"))
        bond_slot_free = sem(name("bond_slot_free"))
        pick_ready = sem(name("pick_ready"))
        pick_used = sem(name("pick_used"))
        gather_ready = sem(name("gather_ready"))
        send_done = sem(name("send_done"))
        send_copied = sem(name("send_copied"))
        if layer == 0:
            x_sb = sb(ctx, name("x_sb"), [128, 2, GROUP], F32)
            outer = sb(ctx, name("outer"), [128, 2, CHUNKS, GROUP], F32)
            x_ps = pb(ctx, name("x_ps"), [128, BANK])
            bond_ps = pb(ctx, name("bond_ps"), [128, CHUNKS, BANK])
            x_spread = sem(name("x_spread"))
            x_copied = sem(name("x_copied"))
            bond_spread = sem(name("bond_spread"))
            outer_done = sem(name("outer_done"))
        else:
            hidden = sb(ctx, name("hidden"), [128, 2, GROUP], F32)
            hidden_ps = pb(ctx, name("hidden_ps"), [HID, 2, BANK])
            hidden_cleared = sem(name("hidden_cleared"))
            hidden_done = sem(name("hidden_done"))
            relu_done = sem(name("relu_done"))

        def sync_part(sp, near):
            row = ROWS_SRC if layer else ROWS_DST_NEAR if near else ROWS_DST
            H = WINDOW if near else NODE_TILES

            def bonds(s, slot):
                start = s * SUPER if isinstance(s, int) else sp.snap(s * SUPER)
                if layer == 0:
                    wait(sp, bond_spread, s * (2 * SUPER_GROUPS) - 2 * SUPER_GROUPS)
                else:
                    wait(sp, hidden_done, s * SUPER_GROUPS - SUPER_GROUPS)
                sp.sem_inc(bond_slot_free, 1)
                sp.dma_start(bond[0:PARTS * BOND, slot, :], bond_tile[:, bass.ds(start, SUPER)]).then_inc(bond_loaded[slot], 16)

            def body(s, slot):
                start = s * SUPER if isinstance(s, int) else sp.snap(s * SUPER)
                wait(sp, pick_ready, (s - 1) * H)
                sp.dma_start(index[:, slot, :], row_table[row:row + 1, bass.ds(start, SUPER)].partition_broadcast(128)).then_inc(index_loaded[slot], 16)
                if isinstance(s, int) and s == 0:
                    sp.wait_ge(bond_cleared, 1)
                else:
                    bonds(s - 1, 1 - slot)
            paired_loop(sp, SUPERS, body)
            bonds(SUPERS - 1, (SUPERS - 1) % 2)

        def vector_part(dve, near):
            H = WINDOW if near else NODE_TILES
            RING = 2 * WINDOW if near else 5

            def picks(s, slot):
                nth = (s + 2) // 2 if isinstance(s, int) else (s - slot) // 2 + 1
                dve.wait_ge(index_loaded[slot], nth * 16)
                for h in range(H):
                    q = s * H + h
                    wait(dve, pick_used, q + 1 - RING)
                    nc.vector.tensor_scalar(pick[:, (slot * H + h) % RING, :], index[:, slot, :], node_id[:, h:h + 1], None,
                                            ALU.is_equal).then_inc(pick_ready, 1)

            def group(i, k):
                for j in range(2):
                    dve.wait_ge(bond_spread, i * 2 + j + 1)
                    dve.wait_ge(x_copied, i + 1)
                    wait(dve, send_done, i - 1)
                    nc.vector.tensor_tensor(outer[:, k, 2 * j:2 * j + 2, :], bond_ps[:, 2 * j:2 * j + 2, 0:GROUP],
                                            x_sb[:, k:k + 1, :].to_broadcast([128, 2, GROUP]), ALU.mult).then_inc(outer_done, 1)

            def body(s, slot):
                back = layer == 0 and not (isinstance(s, int) and s == 0)
                if near:
                    picks(s, slot)
                if back:
                    group(s * 2 - 2, 0)
                if not near:
                    picks(s, slot)
                if back:
                    group(s * 2 - 1, 1)
            paired_loop(dve, SUPERS, body)
            if layer == 0:
                group(GROUPS - 2, 0)
                group(GROUPS - 1, 1)

        def scalar_part(act, near):
            H = WINDOW if near else NODE_TILES

            def evacuate(s, slot):
                act.wait_ge(pick_used, s * H + H)
                wait(act, x_spread if layer == 0 else hidden_done, (s - 1) * SUPER_GROUPS)
                for k in range(SUPER_GROUPS):
                    nc.scalar.activation(gathered[:, slot, k * GROUP:(k + 1) * GROUP], gather_ps[:, k, 0:GROUP], ACT.Copy).then_inc(gather_ready, 1)

            def sent(i):
                act.wait_ge(send_done, i + 1)
                nc.scalar.activation(messages[:, bass.ds(i * GROUP_TILES, GROUP_TILES), :], send_ps[:, :, :], ACT.Copy).then_inc(send_copied, 1)

            def group(i, k):
                if layer == 0:
                    act.wait_ge(x_spread, i + 1)
                    wait(act, send_done, i - 1)
                    wait(act, outer_done, (i - 1) * 2)
                    nc.scalar.activation(x_sb[:, k, :], x_ps[:, 0:GROUP], ACT.Copy).then_inc(x_copied, 1)
                else:
                    act.wait_ge(hidden_done, i + 1)
                    wait(act, send_done, i - 1)
                    nc.scalar.activation(hidden[0:HID, k, :], hidden_ps[:, k, 0:GROUP], ACT.Relu, bias=b1_sb[:, 0:1]).then_inc(relu_done, 1)
                if not (isinstance(i, int) and i == 0):
                    sent(i - 1)

            def body(s, slot):
                if not (isinstance(s, int) and s == 0):
                    group(s * 2 - 2, 0)
                evacuate(s, slot)
                if not (isinstance(s, int) and s == 0):
                    group(s * 2 - 1, 1)
            paired_loop(act, SUPERS, body)
            group(GROUPS - 2, 0)
            group(GROUPS - 1, 1)
            sent(GROUPS - 1)

        def tensor_part(pe, near):
            H = WINDOW if near else NODE_TILES
            RING = 2 * WINDOW if near else 5

            def gather(s, slot):
                wait(pe, gather_ready, s * SUPER_GROUPS)
                if near:
                    first = [pe.value_load(first_tile[0:1, bass.ds(s * SUPER_GROUPS + k, 1)], min_val=0, max_val=NODE_TILES - WINDOW)
                             for k in range(SUPER_GROUPS)]
                for h in range(H):
                    pe.wait_ge(pick_ready, s * H + h + 1)
                    for k in range(SUPER_GROUPS):
                        tile = node_parts[:, bass.ds(first[k] + h, 1), :] if near else node_parts[:, h:h + 1, :]
                        last = nc.tensor.matmul(gather_ps[:, k, 0:GROUP], tile.rearrange("p o c -> p (o c)"),
                                                pick[:, (slot * H + h) % RING, k * GROUP:(k + 1) * GROUP],
                                                start=h == 0, stop=h == H - 1)
                    last.then_inc(pick_used, 1)

            def send_zero(i):
                wait(pe, send_copied, i)
                nc.tensor.matmul(send_ps[:, :, :].rearrange("p t d -> p (t d)"), zeros[:, 0:EDGE_TILE], zeros[:, 0:GROUP_TILES * D],
                                 start=True, stop=False, skip_group_check=True)

            def send_outer(i, k, j):
                pe.wait_ge(outer_done, i * 2 + j + 1)
                for t in range(GROUP_TILES):
                    at = slice(t * EDGE_TILE, (t + 1) * EDGE_TILE)
                    terms = [(outer[:, k, c, at], kernel_sb[:, c, :]) for c in (2 * j, 2 * j + 1)]
                    if j:
                        terms.append((x_sb[:, k, at], bias_sb[:, :]))
                    for left, right in terms:
                        last = nc.tensor.matmul(send_ps[:, t, :], left, right, start=False, stop=False, skip_group_check=True)
                if j:
                    last.then_inc(send_done, 1)

            def send_hidden(i, k):
                pe.wait_ge(relu_done, i + 1)
                wait(pe, send_copied, i)
                for t in range(GROUP_TILES):
                    last = nc.tensor.matmul(send_ps[:, t, :], hidden[:, k, t * EDGE_TILE:(t + 1) * EDGE_TILE], w2_sb[:, :],
                                            start=True, stop=True)
                last.then_inc(send_done, 1)

            def group(i, k, slot, nth):
                first = isinstance(i, int) and i == 0
                here = slice(k * GROUP, (k + 1) * GROUP)
                pe.wait_ge(gather_ready, i + 1)
                pe.wait_ge(bond_loaded[slot], nth * 16)
                if layer == 0:
                    wait(pe, x_copied, i)
                    nc.tensor.matmul(x_ps[:, 0:GROUP], spread_x_sb[:, :], gathered[:, slot, here], start=True, stop=True).then_inc(x_spread, 1)
                    if not first:
                        send_zero(i - 1)
                    for j in range(2):
                        wait(pe, outer_done, i * 2 + j - 1)
                        for c in (2 * j, 2 * j + 1):
                            last = nc.tensor.matmul(bond_ps[:, c, 0:GROUP], spread_bond_sb[:, c, :], bond[:, slot, here], start=True, stop=True)
                        last.then_inc(bond_spread, 1)
                        if not first:
                            send_outer(i - 1, 1 - k, j)
                else:
                    wait(pe, relu_done, i - 1)
                    for part in range(PARTS):
                        nc.tensor.matmul(hidden_ps[:, k, 0:GROUP], w1_node_parts[:, part, :], gathered[:, slot, here], start=part == 0, stop=False)
                        last = nc.tensor.matmul(hidden_ps[:, k, 0:GROUP], w1_edge_parts[:, part, :], bond[0:PARTS * BOND, slot, here],
                                                start=False, stop=part == PARTS - 1)
                    last.then_inc(hidden_done, 1)
                    if not first:
                        send_hidden(i - 1, 1 - k)

            def body(s, slot):
                back = not (isinstance(s, int) and s == 0)
                if back:
                    nth = (s + 1) // 2 if isinstance(s, int) else (s - slot) // 2 + slot
                    group(s * 2 - 2, 0, 1 - slot, nth)
                gather(s, slot)
                if back:
                    group(s * 2 - 1, 1, 1 - slot, nth)
            if layer == 1:
                pe.wait_ge(hidden_cleared, 1)
            paired_loop(pe, SUPERS, body)
            slot = (SUPERS - 1) % 2
            for k in range(SUPER_GROUPS):
                group(GROUPS - 2 + k, k, slot, SUPERS // 2)
            if layer == 0:
                send_zero(GROUPS - 1)
                send_outer(GROUPS - 1, 1, 0)
                send_outer(GROUPS - 1, 1, 1)
            else:
                send_hidden(GROUPS - 1, 1)

        def near_or_far(engine, part):
            if layer == 0:
                flag = engine.value_load(is_near[0:1, 0:1], min_val=0, max_val=1)
                with engine.If(flag > 0):
                    part(engine, True)
                with engine.Else():
                    part(engine, False)
            else:
                part(engine, False)

        with ctx, nc.Block() as block:
            @block.sync
            def _(sp):
                near_or_far(sp, sync_part)

            @block.gpsimd
            def _(pool):
                nc.gpsimd.memset(bond[:, :, :], 0.0).then_inc(bond_cleared, 1)
                if layer == 1:
                    nc.gpsimd.memset(hidden[:, :, :], 0.0).then_inc(hidden_cleared, 1)

            @block.vector
            def _(dve):
                near_or_far(dve, vector_part)

            @block.scalar
            def _(act):
                if layer == 1:
                    act.wait_ge(hidden_cleared, 1)
                near_or_far(act, scalar_part)

            @block.tensor
            def _(pe):
                near_or_far(pe, tensor_part)

    def node_stage(layer):
        ctx = ExitStack()
        name = lambda n: f"{n}_n{layer}"
        RING = 4
        sums_ps = pb(ctx, name("sums_ps"), [COLS, ACC_BANKS * BANK])

        parts_free = sem(name("parts_free"))
        high_done = sem(name("high_done"))
        rest_done = sem(name("rest_done"))
        middle_done = sem(name("middle_done"))
        parts_ready = sem(name("parts_ready"))
        place_ready = sem(name("place_ready"))
        ones_set = sem(name("ones_set"))
        sums_done = sem(name("sums_done"))

        inner = ExitStack()
        parts = sb(inner, name("parts"), [EDGE_TILE, 2, BATCH, COLS], BF16)
        rest = sb(inner, name("rest"), [EDGE_TILE, 2, BATCH, D], F32)
        place = sb(inner, name("place"), [EDGE_TILE, RING, NODES], BF16)

        def vector_part(dve, near):
            column = src_col if layer == 0 else dst_near_col if near else dst_col
            width = WINDOW * NODE_TILE if near else NODES

            def body(s, slot):
                for t in range(BATCH):
                    q = s * BATCH + t
                    wait(dve, parts_free, q + 1 - RING)
                    nc.vector.tensor_scalar(place[:, t % RING, 0:width], node_iota[:, 0:width], column[:, bass.ds(q, 1)], None,
                                            ALU.is_equal).then_inc(place_ready, 1)
            paired_loop(dve, BATCHES, body)

        def tensor_part(pe, near):
            for b in range(ACC_BANKS):
                nc.tensor.matmul(sums_ps[:, b * BANK:(b + 1) * BANK], zeros[0:EDGE_TILE, 0:COLS], zeros[0:EDGE_TILE, :],
                                 start=True, stop=False, skip_group_check=True)
            pe.wait_ge(ones_set, 1)

            def body(s, slot):
                pe.wait_ge(parts_ready, s + 1)
                for t in range(BATCH):
                    if near and t % GROUP_TILES == 0:
                        first = pe.value_load(first_tile[0:1, bass.ds(s * (BATCH // GROUP_TILES) + t // GROUP_TILES, 1)],
                                              min_val=0, max_val=NODE_TILES - WINDOW)
                    pe.wait_ge(place_ready, s * BATCH + t + 1)
                    if near:
                        at = [(bass.ds((first + w) * NODE_TILE, NODE_TILE), slice(w * NODE_TILE, (w + 1) * NODE_TILE)) for w in range(WINDOW)]
                    else:
                        at = [(slice(b, min(b + BANK, N)),) * 2 for b in range(0, N, BANK)]
                    for to, of in at:
                        last = nc.tensor.matmul(sums_ps[:, to], parts[:, slot, t, :], place[:, t % RING, of],
                                                start=False, stop=False, skip_group_check=True)
                    last.then_inc(parts_free, 1)
            paired_loop(pe, BATCHES, body)

        def near_or_far(engine, part):
            if layer == 1:
                flag = engine.value_load(is_near[0:1, 0:1], min_val=0, max_val=1)
                with engine.If(flag > 0):
                    part(engine, True)
                with engine.Else():
                    part(engine, False)
            else:
                part(engine, False)

        with inner, nc.Block() as block:
            @block.gpsimd
            def _(pool):
                nc.gpsimd.memset(parts[:, :, :, COLS - 1:COLS], 1.0).then_inc(ones_set, 1)

                def body(s, slot):
                    pool.wait_ge(high_done, s + 1)
                    wait(pool, middle_done, s - 1)
                    nc.gpsimd.tensor_tensor(rest[:, slot, :, :], messages[:, bass.ds(s * BATCH, BATCH), :], parts[:, slot, :, 0:D],
                                            ALU.subtract).then_inc(rest_done, 1)
                    pool.wait_ge(middle_done, s + 1)
                    nc.gpsimd.tensor_tensor(parts[:, slot, :, 2 * D:3 * D], rest[:, slot, :, :], parts[:, slot, :, D:2 * D],
                                            ALU.subtract).then_inc(parts_ready, 1)
                paired_loop(pool, BATCHES, body)

            @block.scalar
            def _(act):
                def body(s, slot):
                    wait(act, parts_free, (s - 1) * BATCH)
                    wait(act, parts_ready, s - 1)
                    nc.scalar.activation(parts[:, slot, :, 0:D], messages[:, bass.ds(s * BATCH, BATCH), :], ACT.Copy).then_inc(high_done, 1)
                    act.wait_ge(rest_done, s + 1)
                    nc.scalar.activation(parts[:, slot, :, D:2 * D], rest[:, slot, :, :], ACT.Copy).then_inc(middle_done, 1)
                paired_loop(act, BATCHES, body)

            @block.vector
            def _(dve):
                near_or_far(dve, vector_part)

            @block.tensor
            def _(pe):
                near_or_far(pe, tensor_part)

        sums = sb(ctx, name("sums"), [COLS, NODES], F32)
        value = sb(ctx, name("value"), [128, NODE_TILES, D], F32)
        square = sb(ctx, name("square"), [128, NODE_TILES, D], F32)
        stat = sb(ctx, name("stat"), [128, NODE_TILES], F32)
        count = sb(ctx, name("count"), [128, NODE_TILES], F32)
        root = sb(ctx, name("root"), [128, NODE_TILES], F32)
        sums_copied = sem(name("sums_copied"))
        nodes_summed = sem(name("nodes_summed"))
        variance_done = sem(name("variance_done"))
        root_done = sem(name("root_done"))
        node_step = sem(name("node_step"))
        stored = sem(name("stored"))
        HALF = -(-NODE_TILES // 2)
        node_ps = [sums_ps_half for sums_ps_half in (pb(ctx, name("node_ps"), [128, BANK]), None)]

        def node_sums(half):
            n = HALF if half == 0 else NODE_TILES - HALF
            return node_ps[0][:, 0:n * (D + 1)].rearrange("p (h c) -> p h c", c=D + 1), n

        with ctx, nc.Block() as block:
            @block.scalar
            def _(act):
                for b in range(0, ACC_BANKS, 2):
                    at = slice(b * BANK, min((b + 1) * BANK, NODES))
                    nc.scalar.activation(sums[:, at], sums_ps[:, at], ACT.Copy).then_inc(sums_copied, 1)
                act.wait_ge(variance_done, 1)
                nc.scalar.activation(root[:, :], stat[:, :], ACT.Sqrt).then_inc(root_done, 1)

            @block.tensor
            def _(pe):
                pe.wait_ge(sums_copied, ACC_BANKS)
                for half in range(2):
                    to, n = node_sums(half)
                    if half:
                        pe.wait_ge(node_step, 1)
                    for h in range(n):
                        tile = half * HALF + h
                        last = nc.tensor.matmul(to[:, h, :], sums[:, tile * NODE_TILE:(tile + 1) * NODE_TILE], sum_parts_sb[:, :], start=True, stop=True)
                    last.then_inc(nodes_summed, 1)

            @block.vector
            def _(dve):
                v = nc.vector
                done = [0]

                def step(instruction):
                    done[0] += 1
                    instruction.then_inc(node_step, 1)
                    dve.wait_ge(node_step, done[0])

                for b in range(1, ACC_BANKS, 2):
                    at = slice(b * BANK, min((b + 1) * BANK, NODES))
                    v.tensor_copy(sums[:, at], sums_ps[:, at]).then_inc(sums_copied, 1)
                wide = lambda a: a.unsqueeze(2).to_broadcast([128, a.shape[1], D])
                for half in range(2):
                    of, n = node_sums(half)
                    at = slice(half * HALF, half * HALF + n)
                    dve.wait_ge(nodes_summed, half + 1)
                    if layer == 1:
                        v.tensor_scalar(count[:, at], of[:, :, D], 1.0, None, ALU.max)
                        step(v.tensor_copy(value[:, at, :], of[:, :, 0:D])) if half else step(v.tensor_copy(value[:, at, :], of[:, :, 0:D]))
                    else:
                        step(v.tensor_tensor(value[:, at, :], of[:, :, 0:D], node_feats[:, at, :], ALU.add))
                if layer == 1:
                    step(v.reciprocal(count[:, :], count[:, :]))
                    step(v.tensor_tensor(value[:, :, :], value[:, :, :], wide(count[:, :]), ALU.mult))
                    step(v.tensor_tensor(value[:, :, :], value[:, :, :], b2_sb[:, :].unsqueeze(1).to_broadcast([128, NODE_TILES, D]), ALU.add))
                    step(v.tensor_scalar(value[:, :, :], value[:, :, :], 0.0, None, ALU.max))
                    step(v.tensor_tensor(value[:, :, :], value[:, :, :], node_feats[:, :, :], ALU.add))
                step(v.tensor_reduce(stat[:, :], value[:, :, :], AX.X, ALU.add))
                step(v.tensor_scalar(stat[:, :], stat[:, :], 1.0 / D, None, ALU.mult))
                step(v.tensor_tensor(value[:, :, :], value[:, :, :], wide(stat[:, :]), ALU.subtract))
                step(v.tensor_tensor(square[:, :, :], value[:, :, :], value[:, :, :], ALU.mult))
                step(v.tensor_reduce(stat[:, :], square[:, :, :], AX.X, ALU.add))
                step(v.tensor_scalar(stat[:, :], stat[:, :], 1.0 / D, EPS, ALU.mult, ALU.add))
                v.sem_inc(variance_done, 1)
                dve.wait_ge(root_done, 1)
                step(v.reciprocal(root[:, :], root[:, :]))
                step(v.tensor_tensor(node_feats[:, :, :], value[:, :, :], wide(root[:, :]), ALU.mult))
                if layer == 0:
                    split(step, v, [node_parts[:, :, i * D:(i + 1) * D] for i in range(PARTS)], node_feats[:, :, :], square[:, :, :])
                else:
                    v.sem_inc(sums_done, 1)

            @block.sync
            def _(sp):
                if layer == 1:
                    sp.wait_ge(sums_done, 1)
                    sp.dma_start(out[0:FULL * NODE_TILE, :].rearrange("(h p) d -> p h d", p=NODE_TILE), node_feats[:, 0:FULL, :]).then_inc(stored, 16)
                    sp.dma_start(out[FULL * NODE_TILE:N, :], node_feats[0:TAIL, FULL, :]).then_inc(stored, 16)
                    sp.wait_ge(stored, 32)

    message_stage(0)
    node_stage(0)
    message_stage(1)
    node_stage(1)
    top.close()


def laid_out(x, src, dst, edge_attr_16, L0_gnn_kernel, L0_gnn_bias, L1_gnn_W1, L1_gnn_b1, L1_gnn_W2, L1_gnn_b2):
    a = {k: np.asarray(v) for k, v in locals().items()}
    x, src, dst, bond = a["x"], a["src"], a["dst"], a["edge_attr_16"]
    D, E, BOND = x.shape[1], src.shape[0], bond.shape[1]
    nodes = -(-x.shape[0] // NODE_TILE) * NODE_TILE
    row = np.arange(BOND * D) // D
    spread_bond = np.tile(np.arange(BOND)[:, None] == row[None, :], (PARTS, 1)).reshape(PARTS * BOND, -1, 128)
    spread_x = np.tile(np.arange(D)[:, None] == (np.arange(128) % D)[None, :], (PARTS, 1))
    sum_parts = np.zeros((PARTS * D + 1, D + 1), np.float32)
    sum_parts[np.arange(PARTS * D), np.arange(PARTS * D) % D] = 1
    sum_parts[PARTS * D, D] = 1
    laid = dict(
        x=x, src_rows=src, dst_rows=dst, src_cols=src.reshape(-1, EDGE_TILE).T, dst_cols=dst.reshape(-1, EDGE_TILE).T,
        bond_rows=bond.T,
        edge_kernel=a["L0_gnn_kernel"].reshape(BOND, D, D).transpose(0, 2, 1).reshape(-1, 128, D).transpose(1, 0, 2),
        edge_bias=a["L0_gnn_bias"].reshape(D, D).T,
        w1_node=a["L1_gnn_W1"].T[:D], w1_edge=a["L1_gnn_W1"].T[D:], b1=a["L1_gnn_b1"][:, None],
        w2=a["L1_gnn_W2"].T, b2=a["L1_gnn_b2"][None, :],
        node_row=np.arange(nodes, dtype=np.int16)[None, :],
        node_col=np.arange(nodes, dtype=np.float32).reshape(-1, NODE_TILE).T,
        tile_starts=np.arange(0, nodes, NODE_TILE, dtype=np.float32)[None, :],
        spread_bond=spread_bond.astype(np.float32), spread_x=spread_x.astype(np.float32),
        sum_parts=sum_parts)
    return {k: np.ascontiguousarray(v) for k, v in laid.items()}


def kernel(**inputs):
    import concourse.bacc as bacc
    from concourse.bass_utils import run_bass_kernel_spmd

    arrays = laid_out(**inputs)
    nc = bacc.Bacc("TRN2", target_bir_lowering=False, num_devices=1)
    args = {n: nc.dram_tensor(n, v.shape, mybir.dt.from_np(v.dtype), kind="ExternalInput").ap() for n, v in arrays.items()}
    out = nc.dram_tensor("out", arrays["x"].shape, F32, kind="ExternalOutput").ap()
    gnn_program(nc, **args, out=out)
    r = run_bass_kernel_spmd(nc, [arrays], core_ids=[0])
    return r.results[0]["out"]
```

```python
from contextlib import ExitStack

import concourse.bass as bass
import numpy as np
from concourse import mybir

F32 = mybir.dt.float32
F32R = mybir.dt.float32r
BF16 = mybir.dt.bfloat16
I16 = mybir.dt.int16
I32 = mybir.dt.int32
ALU = mybir.AluOpType
ACT = mybir.ActivationFunctionType
AX = mybir.AxisListType

EDGE_TILE = 125
GROUP_TILES = 4
GROUP = EDGE_TILE * GROUP_TILES
SUPER_GROUPS = 2
SUPER = GROUP * SUPER_GROUPS
NODE_TILE = 128
BANK = 512
SPLIT = 2
PARTS = 3
HALVES = 2
QUARTERS = 4
WINDOW = 2
EPS = 1e-5


def wait(engine, semaphore, value):
    if not (isinstance(value, int) and value <= 0):
        engine.wait_ge(semaphore, value)


def first_use(s):
    return isinstance(s, int) and s == 0


def times(s, slot):
    return s // 2 + 1 if isinstance(s, int) else (s - slot) // 2 + 1


def paired_loop(engine, count, body):
    body(0, 0)
    body(1, 1)
    with engine.Fori(1, count // 2) as r:
        body(r * 2, 0)
        body(r * 2 + 1, 1)


def gnn_program(nc, x, src_rows, dst_rows, src_cols, dst_cols, bond_rows, edge_kernel, edge_bias, w1_node, w1_edge,
                b1, w2, b2, node_row, node_col, tile_starts, spread_bond, spread_x, sum_quarters, sum_parts, identity, out):
    N, D = x.shape
    E = src_rows.shape[0]
    BOND = bond_rows.shape[0]
    HID = w1_node.shape[1]
    TILES = E // EDGE_TILE
    GROUPS = E // GROUP
    SUPERS = E // SUPER
    NODE_TILES = -(-N // NODE_TILE)
    FULL = N // NODE_TILE
    TAIL = N - FULL * NODE_TILE
    NODES = NODE_TILES * NODE_TILE
    HALF_TILES = -(-NODE_TILES // HALVES)
    HALF_NODES = HALF_TILES * NODE_TILE
    QUARTER_NODES = NODES // QUARTERS
    TABLE_TILES = HALVES * HALF_TILES
    CHUNKS = BOND * D // 128
    REPEAT = 128 // D
    COLS = PARTS * D + 1
    ACC_BANKS = -(-NODES // BANK)
    ROWS_DST, ROWS_DST_NEAR, ROWS_SRC = range(3)

    top = ExitStack()

    def sb(ctx, name, shape, dt):
        return ctx.enter_context(nc.sbuf_tensor(name, shape, dt))

    def pb(ctx, name, shape, dt=F32):
        return ctx.enter_context(nc.psum_tensor(name, shape, dt))

    def sem(name):
        return top.enter_context(nc.semaphore(name))

    row_table = nc.dram_tensor("row_table", (3, E), I16, kind="Internal").ap()
    half_table = nc.dram_tensor("half_table", (2, HALVES, E), BF16, kind="Internal").ap()
    bond_parts = nc.dram_tensor("bond_parts", (SPLIT, BOND * E), F32, kind="Internal").ap()
    window_table = nc.dram_tensor("window_table", (TABLE_TILES * NODE_TILE, SPLIT * 128), F32, kind="Internal").ap()
    first_tile_f_dram = nc.dram_tensor("first_tile_f_dram", (1, GROUPS), F32, kind="Internal").ap()
    first_dram = nc.dram_tensor("first_dram", (2, GROUPS), I32, kind="Internal").ap()
    spread_dram = nc.dram_tensor("spread_dram", (1, GROUPS), F32, kind="Internal").ap()

    node_feats = sb(top, "node_feats", [128, TABLE_TILES, D], F32)
    pair_parts = sb(top, "pair_parts", [128, HALF_TILES, HALVES, SPLIT, D], F32R)
    node_iota = sb(top, "node_iota", [EDGE_TILE, NODES], I16)
    node_id = sb(top, "node_id", [128, HALF_TILES], F32)
    src_quarter_col = sb(top, "src_quarter_col", [EDGE_TILE, TILES], F32)
    src_quarter = sb(top, "src_quarter", [EDGE_TILE, TILES], BF16)
    dst_col = sb(top, "dst_col", [EDGE_TILE, TILES], F32)
    dst_near_col = sb(top, "dst_near_col", [EDGE_TILE, TILES], F32)
    first = sb(top, "first", [1, 2, GROUPS], I32)
    is_near = sb(top, "is_near", [1, 1], I32)
    kernel_sb = sb(top, "kernel_sb", [128, CHUNKS, D], F32)
    bias_sb = sb(top, "bias_sb", [128, D], F32)
    w1_node_parts = sb(top, "w1_node_parts", [128, SPLIT, 128], F32R)
    w1_edge_parts = sb(top, "w1_edge_parts", [128, SPLIT, 128], F32R)
    b1_sb = sb(top, "b1_sb", [HID, 1], F32)
    w2_sb = sb(top, "w2_sb", [128, D], F32)
    b2_sb = sb(top, "b2_sb", [128, D], F32)
    spread_bond_sb = sb(top, "spread_bond_sb", [128, CHUNKS, 128], F32R)
    spread_x_sb = sb(top, "spread_x_sb", [128, 128], F32R)
    sum_quarters_sb = sb(top, "sum_quarters_sb", [128, 2 * D], F32)
    sum_parts_sb = sb(top, "sum_parts_sb", [COLS, D + 1], F32)
    identity_sb = sb(top, "identity_sb", [128, 128], F32)
    zeros = sb(top, "zeros", [128, BANK], BF16)

    def make_pairs(step, vec):
        for half in range(HALVES):
            whole = node_feats[:, half * HALF_TILES:(half + 1) * HALF_TILES, :]
            step(vec.tensor_copy(pair_parts[:, :, half, 0, :], whole))
            step(vec.tensor_tensor(pair_parts[:, :, half, 1, :], whole, pair_parts[:, :, half, 0, :], ALU.subtract))

    with ExitStack() as ctx:
        PREP = GROUPS // 2
        PER = GROUPS // PREP
        PIECES = 4
        PIECE = BOND * E // (128 * PIECES)
        rows_i = sb(ctx, "rows_i", [PREP, 2, PER * GROUP], I32)
        rows_f = sb(ctx, "rows_f", [PREP, 2, PER * GROUP], F32)
        half_f = sb(ctx, "half_f", [PREP, 2, PER * GROUP], F32)
        pick_16 = sb(ctx, "pick_16", [PREP, 2, PER * GROUP], I16)
        near_16 = sb(ctx, "near_16", [PREP, PER * GROUP], I16)
        halves = sb(ctx, "halves", [PREP, 2, HALVES, PER * GROUP], BF16)
        low = sb(ctx, "low", [PREP, PER], F32)
        high = sb(ctx, "high", [PREP, PER], F32)
        low_tile = sb(ctx, "low_tile", [PREP, PER], F32)
        first_i = sb(ctx, "first_i", [PREP, 2, PER], I32)
        spread = sb(ctx, "spread", [PREP, PER], F32)
        at_least = sb(ctx, "at_least", [PREP, NODE_TILES], F32)
        starts = sb(ctx, "starts", [PREP, NODE_TILES], F32)
        col_i = sb(ctx, "col_i", [EDGE_TILE, 2, TILES], I32)
        col_f = sb(ctx, "col_f", [EDGE_TILE, TILES], F32)
        quarter = sb(ctx, "quarter", [EDGE_TILE, TILES], F32)
        above = sb(ctx, "above", [EDGE_TILE, TILES], F32)
        first_tile_f = sb(ctx, "first_tile_f", [EDGE_TILE, GROUPS], F32)
        spread_row = sb(ctx, "spread_row", [1, GROUPS], F32)
        widest = sb(ctx, "widest", [1, 1], F32)
        x_wide = sb(ctx, "x_wide", [128, TABLE_TILES, SPLIT, REPEAT, D], F32R)
        w_node_f = sb(ctx, "w_node_f", [128, 2, HID], F32)
        w_edge_f = sb(ctx, "w_edge_f", [SPLIT * BOND, 2, HID], F32)
        spread_bond_f = sb(ctx, "spread_bond_f", [SPLIT * BOND, CHUNKS, 128], F32)
        spread_x_f = sb(ctx, "spread_x_f", [128, 128], F32)
        bond_f = sb(ctx, "bond_f", [128, 2, PIECE], F32)
        bond_p = sb(ctx, "bond_p", [128, 2, SPLIT, PIECE], F32R)

        cleared = sem("cleared")
        rows_loaded = sem("rows_loaded")
        cols_loaded = sem("cols_loaded")
        nodes_loaded = sem("nodes_loaded")
        consts_loaded = sem("consts_loaded")
        bond_loaded = [sem(f"bond_loaded{i}") for i in range(2)]
        bond_high = sem("bond_high")
        bond_low = sem("bond_low")
        bond_stored = [sem(f"bond_stored{i}") for i in range(2)]
        tiles_known = sem("tiles_known")
        rows_ready = sem("rows_ready")
        wide_ready = sem("wide_ready")
        prep_stored = sem("prep_stored")
        rows_stored = sem("rows_stored")
        wide_stored = sem("wide_stored")
        near_loaded = sem("near_loaded")
        prep_step = sem("prep_step")

        bond_view = bond_rows.rearrange("b e -> (b e)").rearrange("(p c) -> p c", p=128)
        part_view = bond_parts.rearrange("s (p c) -> p s c", p=128)
        by_prep = lambda row: row.rearrange("(q c) -> q c", q=PREP)
        consts = [(node_iota[:, :], node_row.partition_broadcast(EDGE_TILE)), (node_id[:, :], node_col),
                  (kernel_sb[:, :, :], edge_kernel), (bias_sb[0:D, :], edge_bias), (b1_sb[:, :], b1),
                  (w2_sb[0:HID, :], w2), (b2_sb[:, :], b2.partition_broadcast(128)),
                  (spread_bond_f[:, :, :], spread_bond), (spread_x_f[:, :], spread_x),
                  (sum_quarters_sb[:, :], sum_quarters), (sum_parts_sb[:, :], sum_parts), (identity_sb[:, :], identity)]
        consts += [(w_node_f[i * D:(i + 1) * D, 0, :], w1_node) for i in range(128 // D)]
        consts += [(w_edge_f[i * BOND:(i + 1) * BOND, 0, :], w1_edge) for i in range(SPLIT)]

        with nc.Block() as block:
            @block.sync
            def _(sp):
                sp.dma_start(rows_i[:, 0, :], by_prep(dst_rows)).then_inc(rows_loaded, 16)
                sp.dma_start(rows_i[:, 1, :], by_prep(src_rows)).then_inc(rows_loaded, 16)
                sp.dma_start(starts[:, :], tile_starts.partition_broadcast(PREP)).then_inc(rows_loaded, 16)
                for i in range(PIECES):
                    wait(sp, bond_low, i - 1)
                    sp.dma_start(bond_f[:, i % 2, :], bond_view[:, i * PIECE:(i + 1) * PIECE]).then_inc(bond_loaded[i % 2], 16)
                    if i == 1:
                        sp.dma_start(col_i[:, 0, :], src_cols).then_inc(cols_loaded, 16)
                        sp.dma_start(col_i[:, 1, :], dst_cols).then_inc(cols_loaded, 16)
                        sp.wait_ge(cleared, 1)
                        sp.dma_start(node_feats[:, 0:FULL, :], x[0:FULL * NODE_TILE, :].rearrange("(h p) d -> p h d", p=NODE_TILE)).then_inc(nodes_loaded, 16)
                        sp.dma_start(node_feats[0:TAIL, FULL, :], x[FULL * NODE_TILE:N, :]).then_inc(nodes_loaded, 16)
                for i in range(PIECES):
                    sp.wait_ge(bond_low, i + 1)
                    sp.dma_start(part_view[:, :, i * PIECE:(i + 1) * PIECE], bond_p[:, i % 2, :, :].bitcast(F32)).then_inc(bond_stored[i % 2], 16)
                sp.wait_ge(wide_ready, 1)
                sp.dma_start(window_table.rearrange("(h p) c -> p h c", p=NODE_TILE),
                             x_wide[:, :, :, :, :].rearrange("p h s r d -> p h (s r d)").bitcast(F32)).then_inc(wide_stored, 16)
                for i in range(2):
                    sp.wait_ge(bond_stored[i], 16 * (PIECES // 2))
                sp.wait_ge(wide_stored, 16)

            @block.gpsimd
            def _(pool):
                for t in (node_feats[:, FULL:TABLE_TILES, :], bias_sb[:, :], w2_sb[:, :], spread_bond_sb[:, :, :].bitcast(F32),
                          w1_node_parts[:, :, :].bitcast(F32), w1_edge_parts[:, :, :].bitcast(F32), zeros[:, :]):
                    last = nc.gpsimd.memset(t, 0.0)
                last.then_inc(cleared, 1)
                pool.wait_ge(cleared, 1)
                for to, of in consts:
                    pool.dma_start(to, of).then_inc(consts_loaded, 16)
                pool.wait_ge(consts_loaded, 16 * len(consts))

            @block.scalar
            def _(act):
                def stores():
                    act.wait_ge(tiles_known, 1)
                    act.dma_start(first_tile_f_dram.rearrange("o (q c) -> (o q) c", q=PREP), low_tile[:, :]).then_inc(prep_stored, 16)
                    act.dma_start(first_dram.rearrange("o (q c) -> q o c", q=PREP), first_i[:, :, :]).then_inc(prep_stored, 16)
                    act.dma_start(spread_dram.rearrange("o (q c) -> (o q) c", q=PREP), spread[:, :]).then_inc(prep_stored, 16)
                    act.wait_ge(rows_ready, 1)
                    act.dma_start(by_prep(row_table[ROWS_DST, :]), pick_16[:, 0, :]).then_inc(rows_stored, 16)
                    act.dma_start(by_prep(row_table[ROWS_DST_NEAR, :]), near_16[:, :]).then_inc(rows_stored, 16)
                    act.dma_start(by_prep(row_table[ROWS_SRC, :]), pick_16[:, 1, :]).then_inc(rows_stored, 16)
                    for side in range(2):
                        for half in range(HALVES):
                            act.dma_start(by_prep(half_table[side, half, :]), halves[:, side, half, :]).then_inc(rows_stored, 16)
                    act.wait_ge(prep_stored, 48)
                    act.dma_start(first_tile_f[:, :], first_tile_f_dram.partition_broadcast(EDGE_TILE)).then_inc(near_loaded, 16)
                    act.dma_start(first[:, :, :], first_dram.unsqueeze(0)).then_inc(near_loaded, 16)
                    act.dma_start(spread_row[:, :], spread_dram).then_inc(near_loaded, 16)

                for i in range(PIECES):
                    act.wait_ge(bond_loaded[i % 2], 16 * (i // 2 + 1))
                    if i >= 2:
                        act.wait_ge(bond_stored[i % 2], 16 * (i // 2))
                    nc.scalar.activation(bond_p[:, i % 2, 0, :], bond_f[:, i % 2, :], ACT.Copy).then_inc(bond_high, 1)
                    if i == 1:
                        stores()
                act.wait_ge(rows_stored, 16 * (3 + 2 * HALVES))

            @block.vector
            def _(dve):
                done = [0]

                def step(instruction):
                    done[0] += 1
                    instruction.then_inc(prep_step, 1)
                    dve.wait_ge(prep_step, done[0])

                v = nc.vector

                def bond_piece(i):
                    dve.wait_ge(bond_high, i + 1)
                    v.tensor_tensor(bond_p[:, i % 2, 1, :], bond_f[:, i % 2, :], bond_p[:, i % 2, 0, :], ALU.subtract).then_inc(bond_low, 1)

                dve.wait_ge(rows_loaded, 48)
                step(v.tensor_copy(rows_f[:, :, :], rows_i[:, :, :]))
                groups = rows_f[:, 0, :].rearrange("q (g e) -> q g e", g=PER)
                step(v.tensor_reduce(low[:, :], groups, AX.X, ALU.min))
                step(v.tensor_reduce(high[:, :], groups, AX.X, ALU.max))
                for g in range(PER):
                    step(v.tensor_scalar(at_least[:, 1:NODE_TILES - 1], starts[:, 1:NODE_TILES - 1], low[:, g:g + 1], None,
                                         ALU.is_le, ALU.add, accum_out=low_tile[:, g:g + 1]))
                step(v.tensor_tensor(spread[:, :], high[:, :], low[:, :], ALU.subtract))
                step(v.tensor_copy(first_i[:, 0, :], low_tile[:, :]))
                step(v.tensor_copy(first_i[:, 1, :], low[:, :]))
                v.sem_inc(tiles_known, 1)
                bond_piece(0)
                step(v.tensor_scalar(half_f[:, :, :], rows_f[:, :, :], float(HALF_NODES), None, ALU.is_ge))
                step(v.scalar_tensor_tensor(out=pick_16[:, :, :], in0=half_f[:, :, :], scalar=-float(HALF_NODES), in1=rows_f[:, :, :],
                                            op0=ALU.mult, op1=ALU.add))
                for side in range(2):
                    step(v.tensor_copy(halves[:, side, 1, :], half_f[:, side, :]))
                    step(v.tensor_scalar(halves[:, side, 0, :], half_f[:, side, :], -1.0, 1.0, ALU.mult, ALU.add))
                bond_piece(1)
                for g in range(PER):
                    at = slice(g * GROUP, (g + 1) * GROUP)
                    step(v.tensor_scalar(near_16[:, at], rows_f[:, 0, at], low[:, g:g + 1], None, ALU.subtract))
                v.sem_inc(rows_ready, 1)
                dve.wait_ge(nodes_loaded, 32)
                wide = node_feats[:, :, :].unsqueeze(2).to_broadcast([128, TABLE_TILES, REPEAT, D])
                step(v.tensor_copy(x_wide[:, :, 0, :, :], wide))
                step(v.tensor_tensor(x_wide[:, :, 1, :, :], wide, x_wide[:, :, 0, :, :], ALU.subtract))
                v.sem_inc(wide_ready, 1)
                bond_piece(2)
                bond_piece(3)
                dve.wait_ge(cols_loaded, 32)
                step(v.tensor_copy(col_f[:, :], col_i[:, 0, :]))
                step(v.tensor_scalar(quarter[:, :], col_f[:, :], float(QUARTER_NODES), None, ALU.is_ge))
                for q in range(2, QUARTERS):
                    step(v.tensor_scalar(above[:, :], col_f[:, :], float(q * QUARTER_NODES), None, ALU.is_ge))
                    step(v.tensor_tensor(quarter[:, :], quarter[:, :], above[:, :], ALU.add))
                step(v.scalar_tensor_tensor(out=src_quarter_col[:, :], in0=quarter[:, :], scalar=-float(QUARTER_NODES), in1=col_f[:, :],
                                            op0=ALU.mult, op1=ALU.add))
                step(v.tensor_copy(src_quarter[:, :], quarter[:, :]))
                step(v.tensor_copy(dst_col[:, :], col_i[:, 1, :]))
                dve.wait_ge(near_loaded, 48)
                step(v.tensor_scalar(first_tile_f[:, :], first_tile_f[:, :], float(NODE_TILE), None, ALU.mult))
                step(v.tensor_tensor(dst_near_col[:, :].rearrange("p (g t) -> p g t", g=GROUPS),
                                     dst_col[:, :].rearrange("p (g t) -> p g t", g=GROUPS),
                                     first_tile_f[:, :].unsqueeze(2).to_broadcast([EDGE_TILE, GROUPS, GROUP_TILES]), ALU.subtract))
                step(v.tensor_reduce(widest[:, :], spread_row[:, :], AX.X, ALU.max))
                step(v.tensor_scalar(is_near[:, :], widest[:, :], float(NODE_TILE - 1), None, ALU.is_le))
                make_pairs(step, v)
                dve.wait_ge(consts_loaded, 16 * len(consts))
                step(v.tensor_copy(spread_bond_sb[0:SPLIT * BOND, :, :], spread_bond_f[:, :, :]))
                step(v.tensor_copy(spread_x_sb[:, :], spread_x_f[:, :]))
                for parts, whole in ((w1_node_parts[:, :, 0:HID], w_node_f), (w1_edge_parts[0:SPLIT * BOND, :, 0:HID], w_edge_f)):
                    step(v.tensor_copy(parts[:, 0, :], whole[:, 0, :]))
                    step(v.tensor_tensor(parts[:, 1, :], whole[:, 0, :], parts[:, 0, :], ALU.subtract))

    messages = sb(top, "messages", [EDGE_TILE, TILES, D], F32)
    bond_tile = bond_parts.rearrange("s (b e) -> (s b) e", b=BOND)

    def message_stage(layer):
        ctx = ExitStack()
        name = lambda n: f"{n}_m{layer}"
        RING = 6 if layer else 4
        BANKS = 2 if layer else 1
        index = sb(ctx, name("index"), [128, 2, SUPER], I16)
        mask = sb(ctx, name("mask"), [128, 2, SUPER], BF16)
        bond = sb(ctx, name("bond"), [128, 2, SUPER], F32R)
        pick = sb(ctx, name("pick"), [128, RING + 1, SUPER], F32R)
        raw = sb(ctx, name("raw"), [128, 2, SUPER], F32)
        gathered = sb(ctx, name("gathered"), [128, 2, SUPER], F32R)
        turned = sb(ctx, name("turned"), [128, 2, EDGE_TILE], F32)
        gather_ps = pb(ctx, name("gather_ps"), [128, BANKS * SUPER_GROUPS, BANK])
        turned_ps = pb(ctx, name("turned_ps"), [128, BANK])
        send_ps = pb(ctx, name("send_ps"), [EDGE_TILE, BANK])

        index_loaded = [sem(name(f"index_loaded{i}")) for i in range(2)]
        mask_loaded = [sem(name(f"mask_loaded{i}")) for i in range(2)]
        bond_loaded = [sem(name(f"bond_loaded{i}")) for i in range(2)]
        bond_cleared = sem(name("bond_cleared"))
        slot_free = sem(name("slot_free"))
        first_ready = sem(name("first_ready"))
        first_free = sem(name("first_free"))
        pick_ready = sem(name("pick_ready"))
        pick_used = sem(name("pick_used"))
        raw_ready = sem(name("raw_ready"))
        gather_ready = sem(name("gather_ready"))
        turned_done = sem(name("turned_done"))
        turned_copied = sem(name("turned_copied"))
        send_done = sem(name("send_done"))
        send_copied = sem(name("send_copied"))
        if layer == 0:
            window = gathered[:, :, :].rearrange("p a e -> p (a e)")[:, 0:2 * SUPER_GROUPS * SPLIT * 128].rearrange(
                "p (g s c) -> p g s c", s=SPLIT, c=128)
            x_sb = sb(ctx, name("x_sb"), [128, 2, GROUP], F32)
            outer = sb(ctx, name("outer"), [128, 2, CHUNKS, GROUP], F32)
            bond_ps = pb(ctx, name("bond_ps"), [128, CHUNKS, BANK])
            window_loaded = [sem(name(f"window_loaded{i}")) for i in range(2 * SUPER_GROUPS)]
            x_spread = sem(name("x_spread"))
            x_copied = sem(name("x_copied"))
            bond_spread = sem(name("bond_spread"))
            outer_done = sem(name("outer_done"))
            features_used = x_spread
        else:
            hidden = sb(ctx, name("hidden"), [128, 2, GROUP], F32)
            hidden_ps = pb(ctx, name("hidden_ps"), [128, 2, BANK])
            hidden_cleared = sem(name("hidden_cleared"))
            hidden_done = sem(name("hidden_done"))
            relu_done = sem(name("relu_done"))
            features_used = hidden_done

        def pick_slot(h):
            return RING if h == 0 else (h - 1) % RING

        def pick_before(q, h):
            return q + 1 - (HALF_TILES if h == 0 else RING if h > RING else RING + 1)

        def in_order(s, slot, front, group):
            front(s, slot)
            if layer == 0:
                for k in range(SUPER_GROUPS):
                    group(s * 2 + k, k, s, slot)

        def sync_part(sp, near):
            row = ROWS_SRC if layer else ROWS_DST_NEAR if near else ROWS_DST
            H = 1 if near else HALF_TILES - 1

            def body(s, slot):
                start = s * SUPER if isinstance(s, int) else sp.snap(s * SUPER)
                if near:
                    lowest = [sp.value_load(first[0:1, 1, bass.ds(s * SUPER_GROUPS + k, 1)], min_val=0, max_val=(TABLE_TILES - 1) * NODE_TILE)
                              for k in range(SUPER_GROUPS)]
                wait(sp, pick_ready, s * H - H)
                if not near:
                    sp.sem_inc(slot_free, 1)
                    wait(sp, first_ready, s - 1)
                sp.sem_inc(slot_free, 1)
                sp.dma_start(index[:, slot, :], row_table[row:row + 1, bass.ds(start, SUPER)].partition_broadcast(128)).then_inc(index_loaded[slot], 16)
                if near:
                    wait(sp, x_spread, s * SUPER_GROUPS - SUPER_GROUPS)
                    sp.sem_inc(slot_free, 1)
                    for k in range(SUPER_GROUPS):
                        at = slot * SUPER_GROUPS + k
                        sp.dma_start(window[:, at, :, :].rearrange("p s c -> p (s c)").bitcast(F32),
                                     window_table[bass.ds(lowest[k], NODE_TILE), :]).then_inc(window_loaded[at], 16)
                else:
                    wait(sp, gather_ready, s * SUPER_GROUPS - SUPER_GROUPS)
                    sp.sem_inc(slot_free, 1)
                    for half in range(HALVES):
                        sp.dma_start(mask[half * 64:half * 64 + 64, slot, :],
                                     half_table[layer, half:half + 1, bass.ds(start, SUPER)].partition_broadcast(64)).then_inc(mask_loaded[slot], 16)
                if first_use(s):
                    sp.wait_ge(bond_cleared, 1)
                elif layer == 0:
                    wait(sp, bond_spread, s * (2 * SUPER_GROUPS) - 2 * SUPER_GROUPS)
                else:
                    wait(sp, hidden_done, s * SUPER_GROUPS - SUPER_GROUPS)
                sp.sem_inc(slot_free, 1)
                sp.dma_start(bond[0:SPLIT * BOND, slot, :].bitcast(F32), bond_tile[:, bass.ds(start, SUPER)]).then_inc(bond_loaded[slot], 16)
            paired_loop(sp, SUPERS, body)

        def vector_part(dve, near):
            H = 1 if near else HALF_TILES

            def picks(s, slot):
                dve.wait_ge(index_loaded[slot], times(s, slot) * 16)
                for h in range(0 if near else 1, H):
                    if near:
                        wait(dve, x_spread, s * SUPER_GROUPS - SUPER_GROUPS)
                    else:
                        wait(dve, pick_used, pick_before(s * H + h, h))
                    nc.vector.tensor_scalar(pick[:, slot if near else pick_slot(h), :], index[:, slot, :], node_id[:, h:h + 1], None,
                                            ALU.is_equal).then_inc(pick_ready, 1)

            def group(i, k, s, slot):
                for j in range(2):
                    dve.wait_ge(bond_spread, i * 2 + j + 1)
                    dve.wait_ge(x_copied, i + 1)
                    wait(dve, turned_done, i - 1)
                    nc.vector.tensor_tensor(outer[:, k, 2 * j:2 * j + 2, :], bond_ps[:, 2 * j:2 * j + 2, 0:GROUP],
                                            x_sb[:, k:k + 1, :].to_broadcast([128, 2, GROUP]), ALU.mult).then_inc(outer_done, 1)

            def body(s, slot):
                if layer == 1:
                    picks(s, slot)
                elif near:
                    picks(s, slot)
                    if not first_use(s):
                        for k in range(SUPER_GROUPS):
                            group(s * 2 - 2 + k, k, s - 1, 1 - slot)
                else:
                    in_order(s, slot, picks, group)
            paired_loop(dve, SUPERS, body)
            if near:
                for k in range(SUPER_GROUPS):
                    group(GROUPS - SUPER_GROUPS + k, k, SUPERS - 1, (SUPERS - 1) % 2)

        def scalar_part(act, near):
            H = 1 if near else HALF_TILES

            def evacuate(s, slot):
                if near:
                    return
                act.wait_ge(pick_used, s * H + H)
                wait(act, gather_ready, s * SUPER_GROUPS - SUPER_GROUPS)
                for k in range(SUPER_GROUPS):
                    of = slot * SUPER_GROUPS + k if BANKS == 2 else k
                    nc.scalar.activation(raw[:, slot, k * GROUP:(k + 1) * GROUP], gather_ps[:, of, 0:GROUP], ACT.Copy).then_inc(raw_ready, 1)

            def copy_turned(i, k):
                act.wait_ge(turned_done, i + 1)
                wait(act, send_done, i - 1)
                nc.scalar.activation(turned[:, k, :], turned_ps[:, 0:EDGE_TILE], ACT.Copy).then_inc(turned_copied, 1)

            def copy_sent(i):
                act.wait_ge(send_done, i + 1)
                nc.scalar.activation(messages[:, bass.ds(i * GROUP_TILES, GROUP_TILES), :],
                                     send_ps[:, 0:GROUP_TILES * D].rearrange("p (t d) -> p t d", d=D), ACT.Copy).then_inc(send_copied, 1)

            def relu(i, k):
                act.wait_ge(hidden_done, i + 1)
                wait(act, turned_done, i - 1)
                nc.scalar.activation(hidden[0:HID, k, :], hidden_ps[0:HID, k, 0:GROUP], ACT.Relu, bias=b1_sb[:, 0:1]).then_inc(relu_done, 1)

            def finish(s, slot):
                for of_group in (relu, copy_turned, lambda i, k: copy_sent(i)):
                    for k in range(SUPER_GROUPS):
                        of_group(s * 2 + k, k)

            def body_1(s, slot):
                if not first_use(s):
                    finish(s - 1, 1 - slot)
                evacuate(s, slot)

            def group(i, k, s, slot):
                act.wait_ge(x_spread, i + 1)
                wait(act, turned_done, i - 1)
                wait(act, outer_done, i * 2 - 2)
                nc.scalar.activation(x_sb[:, k, :], gather_ps[:, k, 0:GROUP], ACT.Copy).then_inc(x_copied, 1)
                if not (isinstance(i, int) and i < 1):
                    copy_turned(i - 1, 1 - k)
                if not (isinstance(i, int) and i < 2):
                    copy_sent(i - 2)

            if layer == 1:
                paired_loop(act, SUPERS, body_1)
                finish(SUPERS - 1, 1)
                return
            paired_loop(act, SUPERS, lambda s, slot: in_order(s, slot, evacuate, group))
            copy_turned(GROUPS - 1, 1)
            copy_sent(GROUPS - 2)
            copy_sent(GROUPS - 1)

        def tensor_part(pe, near):
            H = 1 if near else HALF_TILES

            def gather(s, slot):
                if near:
                    return
                if BANKS == 2:
                    wait(pe, raw_ready, s * SUPER_GROUPS - SUPER_GROUPS)
                else:
                    wait(pe, x_copied, s * SUPER_GROUPS)
                for h in range(H):
                    if h == 0:
                        pe.wait_ge(first_ready, s + 1)
                    else:
                        pe.wait_ge(pick_ready, s * (H - 1) + h)
                    for k in range(SUPER_GROUPS):
                        to = slot * SUPER_GROUPS + k if BANKS == 2 else k
                        last = nc.tensor.matmul(gather_ps[:, to, 0:GROUP], pair_parts[:, h, :, :, :].rearrange("p a s d -> p (a s d)"),
                                                pick[:, pick_slot(h), k * GROUP:(k + 1) * GROUP], start=h == 0, stop=h == H - 1)
                    last.then_inc(pick_used, 1)
                    if layer == 1 and not first_use(s):
                        finish(s - 1, 1 - slot, h)

            def turn(i, k, terms):
                for n, (left, right, start, stop) in enumerate(terms):
                    for t in range(GROUP_TILES):
                        last = nc.tensor.matmul(turned_ps[t * D:(t + 1) * D, 0:EDGE_TILE], left, right[:, t * EDGE_TILE:(t + 1) * EDGE_TILE],
                                                start=start, stop=stop, skip_group_check=True)
                return last

            def turn_outer(i, k, j):
                if j == 0:
                    wait(pe, turned_copied, i)
                pe.wait_ge(outer_done, i * 2 + j + 1)
                terms = [(kernel_sb[:, c, :], outer[:, k, c, :], c == 0, False) for c in (2 * j, 2 * j + 1)]
                if j:
                    terms.append((bias_sb[:, :], x_sb[:, k, :], False, True))
                last = turn(i, k, terms)
                if j:
                    last.then_inc(turned_done, 1)

            def turn_hidden(i, k):
                pe.wait_ge(relu_done, i + 1)
                wait(pe, turned_copied, i)
                turn(i, k, [(w2_sb[:, :], hidden[:, k, :], True, True)]).then_inc(turned_done, 1)

            def send(i, k):
                pe.wait_ge(turned_copied, i + 1)
                wait(pe, send_copied, i)
                nc.tensor.matmul(send_ps[:, 0:128], turned[:, k, :], identity_sb[:, :], start=True, stop=True).then_inc(send_done, 1)

            def hide(i, k, s, slot):
                here = slice(k * GROUP, (k + 1) * GROUP)
                pe.wait_ge(gather_ready, i + 1)
                pe.wait_ge(bond_loaded[slot], times(s, slot) * 16)
                wait(pe, relu_done, i - 1)
                for part in range(SPLIT):
                    nc.tensor.matmul(hidden_ps[:, k, 0:GROUP], w1_node_parts[:, part, :], gathered[:, slot, here], start=part == 0, stop=False)
                    last = nc.tensor.matmul(hidden_ps[:, k, 0:GROUP], w1_edge_parts[:, part, :], bond[:, slot, here],
                                            start=False, stop=part == SPLIT - 1)
                last.then_inc(hidden_done, 1)

            def finish(s, slot, h):
                i = s * 2
                if h == 5:
                    hide(i, 0, s, slot)
                elif h == 7:
                    hide(i + 1, 1, s, slot)
                    turn_hidden(i, 0)
                elif h == 9:
                    turn_hidden(i + 1, 1)
                    send(i, 0)
                elif h == 11:
                    send(i + 1, 1)

            def group(i, k, s, slot):
                here = slice(k * GROUP, (k + 1) * GROUP)
                if near:
                    at = slot * SUPER_GROUPS + k
                    pe.wait_ge(window_loaded[at], times(s, slot) * 16)
                    pe.wait_ge(pick_ready, s + 1)
                    wait(pe, x_copied, i - 1)
                    for part in range(SPLIT):
                        last = nc.tensor.matmul(gather_ps[:, k, 0:GROUP], window[:, at, part, :], pick[:, slot, here],
                                                start=part == 0, stop=part == SPLIT - 1)
                else:
                    pe.wait_ge(gather_ready, i + 1)
                    last = nc.tensor.matmul(gather_ps[:, k, 0:GROUP], spread_x_sb[:, :], gathered[:, slot, here], start=True, stop=True)
                last.then_inc(x_spread, 1)
                pe.wait_ge(bond_loaded[slot], times(s, slot) * 16)
                for j in range(2):
                    wait(pe, outer_done, i * 2 + j - 1)
                    for c in (2 * j, 2 * j + 1):
                        last = nc.tensor.matmul(bond_ps[:, c, 0:GROUP], spread_bond_sb[:, c, :], bond[:, slot, here], start=True, stop=True)
                    last.then_inc(bond_spread, 1)
                    if j == 0 and not (isinstance(i, int) and i < 2):
                        send(i - 2, k)
                    if not (isinstance(i, int) and i < 1):
                        turn_outer(i - 1, 1 - k, j)

            if layer == 1:
                pe.wait_ge(hidden_cleared, 1)
                paired_loop(pe, SUPERS, gather)
                for h in range(H):
                    finish(SUPERS - 1, 1, h)
                return
            paired_loop(pe, SUPERS, lambda s, slot: in_order(s, slot, gather, group))
            send(GROUPS - 2, 0)
            turn_outer(GROUPS - 1, 1, 0)
            turn_outer(GROUPS - 1, 1, 1)
            send(GROUPS - 1, 1)

        def pool_part(pool, near):
            def first_pick(s, slot):
                pool.wait_ge(index_loaded[slot], times(s, slot) * 16)
                wait(pool, pick_used, pick_before(s * HALF_TILES, 0))
                pool.sem_inc(first_free, 1)
                nc.gpsimd.tensor_scalar(pick[:, pick_slot(0), :], index[:, slot, :], node_id[:, 0:1], None, ALU.is_equal).then_inc(first_ready, 1)

            def clear_half(s, slot):
                pool.wait_ge(mask_loaded[slot], times(s, slot) * 16 * HALVES)
                wait(pool, features_used, s * SUPER_GROUPS - SUPER_GROUPS)
                for k in range(SUPER_GROUPS):
                    here = slice(k * GROUP, (k + 1) * GROUP)
                    pool.wait_ge(raw_ready, s * SUPER_GROUPS + k + 1)
                    nc.gpsimd.tensor_tensor(gathered[:, slot, here], raw[:, slot, here], mask[:, slot, here], ALU.mult).then_inc(gather_ready, 1)

            def body(s, slot):
                first_pick(s, slot)
                if not first_use(s):
                    clear_half(s - 1, 1 - slot)

            if not near:
                paired_loop(pool, SUPERS, body)
                clear_half(SUPERS - 1, 1)

        def near_or_far(engine, part):
            if layer == 0:
                flag = engine.value_load(is_near[0:1, 0:1], min_val=0, max_val=1)
                with engine.If(flag > 0):
                    part(engine, True)
                with engine.Else():
                    part(engine, False)
            else:
                part(engine, False)

        with ctx, nc.Block() as block:
            @block.sync
            def _(sp):
                near_or_far(sp, sync_part)

            @block.gpsimd
            def _(pool):
                nc.gpsimd.memset(bond[:, :, :].bitcast(F32), 0.0).then_inc(bond_cleared, 1)
                if layer == 1:
                    nc.gpsimd.memset(hidden[:, :, :], 0.0).then_inc(hidden_cleared, 1)
                near_or_far(pool, pool_part)

            @block.vector
            def _(dve):
                near_or_far(dve, vector_part)

            @block.scalar
            def _(act):
                if layer == 1:
                    act.wait_ge(hidden_cleared, 1)
                near_or_far(act, scalar_part)

            @block.tensor
            def _(pe):
                near_or_far(pe, tensor_part)

    def normalize(dve, step, layer, value, square, stat, root, variance_done, root_done):
        v = nc.vector
        wide = lambda a: a.unsqueeze(2).to_broadcast([128, NODE_TILES, D])
        step(v.tensor_reduce(stat[:, :], value[:, :, :], AX.X, ALU.add))
        step(v.tensor_scalar(stat[:, :], stat[:, :], 1.0 / D, None, ALU.mult))
        step(v.tensor_tensor(value[:, :, :], value[:, :, :], wide(stat[:, :]), ALU.subtract))
        step(v.tensor_tensor(square[:, :, :], value[:, :, :], value[:, :, :], ALU.mult))
        step(v.tensor_reduce(stat[:, :], square[:, :, :], AX.X, ALU.add))
        step(v.tensor_scalar(stat[:, :], stat[:, :], 1.0 / D, EPS, ALU.mult, ALU.add))
        v.sem_inc(variance_done, 1)
        dve.wait_ge(root_done, 1)
        step(v.reciprocal(root[:, :], root[:, :]))
        step(v.tensor_tensor(node_feats[:, 0:NODE_TILES, :], value[:, :, :], wide(root[:, :]), ALU.mult))

    def source_stage():
        ctx = ExitStack()
        RING = 4
        BATCH = 8
        BATCHES = TILES // BATCH
        SETS = QUARTERS // 2
        sums_ps = pb(ctx, "src_sums_ps", [128, SETS, 2 * BANK])
        node_ps = pb(ctx, "src_node_ps", [128, 2, BANK])
        place_used = sem("src_place_used")
        place_ready = sem("src_place_ready")
        high_done = sem("src_high_done")
        low_done = sem("src_low_done")
        masked_done = sem("src_masked_done")

        inner = ExitStack()
        parts = sb(inner, "src_parts", [EDGE_TILE, 2, BATCH, SPLIT * D], F32R)
        masked = sb(inner, "src_masked", [EDGE_TILE, 2, BATCH, QUARTERS, SPLIT * D], F32R)
        place = sb(inner, "src_place", [EDGE_TILE, RING, QUARTER_NODES], F32R)
        quarter_mask = sb(inner, "src_quarter_mask", [EDGE_TILE, TILES, QUARTERS], BF16)
        quarters_known = sem("src_quarters_known")
        with inner, nc.Block() as block:
            @block.scalar
            def _(act):
                def body(s, slot):
                    wait(act, masked_done, s - 1)
                    nc.scalar.activation(parts[:, slot, :, 0:D], messages[:, bass.ds(s * BATCH, BATCH), :], ACT.Copy).then_inc(high_done, 1)
                paired_loop(act, BATCHES, body)

            @block.gpsimd
            def _(pool):
                def body(s, slot):
                    if first_use(s):
                        pool.wait_ge(quarters_known, QUARTERS)
                    """Each edge's parts once for each quarter, cleared but for the quarter of its src."""
                    pool.wait_ge(high_done, s + 1)
                    nc.gpsimd.tensor_tensor(parts[:, slot, :, D:2 * D], messages[:, bass.ds(s * BATCH, BATCH), :], parts[:, slot, :, 0:D],
                                            ALU.subtract).then_inc(low_done, 1)
                    pool.wait_ge(low_done, s + 1)
                    wait(pool, place_used, s * BATCH - BATCH)
                    shape = [EDGE_TILE, BATCH, QUARTERS, SPLIT * D]
                    nc.gpsimd.tensor_tensor(masked[:, slot, :, :, :], parts[:, slot, :, :].unsqueeze(2).to_broadcast(shape),
                                            quarter_mask[:, bass.ds(s * BATCH, BATCH), :].unsqueeze(3).to_broadcast(shape), ALU.mult).then_inc(masked_done, 1)
                paired_loop(pool, BATCHES, body)

            @block.vector
            def _(dve):
                for q in range(QUARTERS):
                    nc.vector.tensor_scalar(quarter_mask[:, :, q], src_quarter[:, :], float(q), None, ALU.is_equal).then_inc(quarters_known, 1)

                def body(s, slot):
                    for t in range(BATCH):
                        wait(dve, place_used, s * BATCH + t + 1 - RING)
                        nc.vector.tensor_scalar(place[:, t % RING, :], node_iota[:, 0:QUARTER_NODES], src_quarter_col[:, bass.ds(s * BATCH + t, 1)],
                                                None, ALU.is_equal).then_inc(place_ready, 1)
                paired_loop(dve, BATCHES, body)

            @block.tensor
            def _(pe):
                spans = [(b, min(b + BANK, QUARTER_NODES)) for b in range(0, QUARTER_NODES, BANK)]
                for a in range(SETS):
                    for lo, hi in spans:
                        nc.tensor.matmul(sums_ps[:, a, lo:hi], zeros[0:EDGE_TILE, 0:128], zeros[0:EDGE_TILE, 0:hi - lo],
                                         start=True, stop=False, skip_group_check=True)

                def body(s, slot):
                    pe.wait_ge(masked_done, s + 1)
                    for t in range(BATCH):
                        pe.wait_ge(place_ready, s * BATCH + t + 1)
                        for a in range(SETS):
                            for lo, hi in spans:
                                last = nc.tensor.matmul(sums_ps[:, a, lo:hi], masked[:, slot, t, 2 * a:2 * a + 2, :].rearrange("p q c -> p (q c)"),
                                                        place[:, t % RING, lo:hi], start=False, stop=False, skip_group_check=True)
                        last.then_inc(place_used, 1)
                paired_loop(pe, BATCHES, body)

        BANK_TILES = BANK // D

        def pieces(h):
            for size in (NODE_TILE, NODE_TILE // QUARTERS):
                cut = [((h * NODE_TILE + at) // QUARTER_NODES, at, size) for at in range(0, NODE_TILE, size)]
                if all(h * NODE_TILE + at + n <= (q + 1) * QUARTER_NODES for q, at, n in cut):
                    return cut

        sums = sb(ctx, "src_sums", [128, SETS, QUARTER_NODES], F32)
        value = sb(ctx, "src_value", [128, NODE_TILES, D], F32)
        square = sb(ctx, "src_square", [128, NODE_TILES, D], F32)
        stat = sb(ctx, "src_stat", [128, NODE_TILES], F32)
        root = sb(ctx, "src_root", [128, NODE_TILES], F32)
        sums_copied = sem("src_sums_copied")
        nodes_summed = sem("src_nodes_summed")
        variance_done = sem("src_variance_done")
        root_done = sem("src_root_done")
        node_step = sem("src_node_step")
        with ctx, nc.Block() as block:
            @block.scalar
            def _(act):
                nc.scalar.activation(sums[:, 0, :], sums_ps[:, 0, 0:QUARTER_NODES], ACT.Copy).then_inc(sums_copied, 1)
                act.wait_ge(variance_done, 1)
                nc.scalar.activation(root[:, :], stat[:, :], ACT.Sqrt).then_inc(root_done, 1)

            @block.tensor
            def _(pe):
                pe.wait_ge(sums_copied, 2)
                for b in range(2):
                    for h in range(b * BANK_TILES, min((b + 1) * BANK_TILES, NODE_TILES)):
                        for q, at, n in pieces(h):
                            last = nc.tensor.matmul(node_ps[at:at + n, b, (h % BANK_TILES) * D:(h % BANK_TILES + 1) * D],
                                                    sums[:, q // 2, h * NODE_TILE + at - q * QUARTER_NODES:][:, 0:n],
                                                    sum_quarters_sb[:, (q % 2) * D:(q % 2 + 1) * D], start=True, stop=True)
                    last.then_inc(nodes_summed, 1)

            @block.vector
            def _(dve):
                v = nc.vector
                done = [0]

                def step(instruction):
                    done[0] += 1
                    instruction.then_inc(node_step, 1)
                    dve.wait_ge(node_step, done[0])

                v.tensor_copy(sums[:, 1, :], sums_ps[:, 1, 0:QUARTER_NODES]).then_inc(sums_copied, 1)
                for b in range(2):
                    dve.wait_ge(nodes_summed, b + 1)
                    at = slice(b * BANK_TILES, min((b + 1) * BANK_TILES, NODE_TILES))
                    of = node_ps[:, b, 0:(at.stop - at.start) * D].rearrange("p (h d) -> p h d", d=D)
                    step(v.tensor_tensor(value[:, at, :], of, node_feats[:, at, :], ALU.add))
                normalize(dve, step, 0, value, square, stat, root, variance_done, root_done)
                make_pairs(step, v)

    def target_stage():
        ctx = ExitStack()
        name = lambda n: f"dst_{n}"
        RING = 5
        BATCH = 40
        BATCHES = TILES // BATCH
        sums_ps = pb(ctx, name("sums_ps"), [COLS, ACC_BANKS * BANK])

        parts_free = sem(name("parts_free"))
        high_done = sem(name("high_done"))
        rest_done = sem(name("rest_done"))
        middle_done = sem(name("middle_done"))
        parts_ready = sem(name("parts_ready"))
        place_ready = sem(name("place_ready"))
        ones_set = sem(name("ones_set"))
        sums_done = sem(name("sums_done"))

        inner = ExitStack()
        parts = sb(inner, name("parts"), [EDGE_TILE, 2, BATCH, COLS], BF16)
        rest = sb(inner, name("rest"), [EDGE_TILE, 2, BATCH, D], F32)
        place = sb(inner, name("place"), [EDGE_TILE, RING, NODES], BF16)

        def vector_part(dve, near):
            column = dst_near_col if near else dst_col
            width = WINDOW * NODE_TILE if near else NODES

            def body(s, slot):
                for t in range(BATCH):
                    q = s * BATCH + t
                    wait(dve, parts_free, q + 1 - RING)
                    nc.vector.tensor_scalar(place[:, t % RING, 0:width], node_iota[:, 0:width], column[:, bass.ds(q, 1)], None,
                                            ALU.is_equal).then_inc(place_ready, 1)
            paired_loop(dve, BATCHES, body)

        def tensor_part(pe, near):
            for b in range(ACC_BANKS):
                nc.tensor.matmul(sums_ps[:, b * BANK:(b + 1) * BANK], zeros[0:EDGE_TILE, 0:COLS], zeros[0:EDGE_TILE, :],
                                 start=True, stop=False, skip_group_check=True)
            pe.wait_ge(ones_set, 1)

            def body(s, slot):
                if near:
                    _, lowest = nc.values_load_multi_w_load_instructions(first[0:1, 0, bass.ds(s * (BATCH // GROUP_TILES), BATCH // GROUP_TILES)],
                                                                         engines=[mybir.EngineType.PE], min_val=0, max_val=NODE_TILES - WINDOW,
                                                                         skip_runtime_bounds_check_because="it counts tiles 1 .. NODE_TILES - WINDOW")
                pe.wait_ge(parts_ready, s + 1)
                for t in range(BATCH):
                    pe.wait_ge(place_ready, s * BATCH + t + 1)
                    if near:
                        at = [(bass.ds((lowest[t // GROUP_TILES] + w) * NODE_TILE, NODE_TILE), slice(w * NODE_TILE, (w + 1) * NODE_TILE)) for w in range(WINDOW)]
                    else:
                        at = [(slice(b, min(b + BANK, N)),) * 2 for b in range(0, N, BANK)]
                    for to, of in at:
                        last = nc.tensor.matmul(sums_ps[:, to], parts[:, slot, t, :], place[:, t % RING, of],
                                                start=False, stop=False, skip_group_check=True)
                    last.then_inc(parts_free, 1)
            paired_loop(pe, BATCHES, body)

        def near_or_far(engine, part):
            flag = engine.value_load(is_near[0:1, 0:1], min_val=0, max_val=1)
            with engine.If(flag > 0):
                part(engine, True)
            with engine.Else():
                part(engine, False)

        with inner, nc.Block() as block:
            @block.gpsimd
            def _(pool):
                nc.gpsimd.memset(parts[:, :, :, COLS - 1:COLS], 1.0).then_inc(ones_set, 1)

                def body(s, slot):
                    pool.wait_ge(high_done, s + 1)
                    nc.gpsimd.tensor_tensor(rest[:, slot, :, :], messages[:, bass.ds(s * BATCH, BATCH), :], parts[:, slot, :, 0:D],
                                            ALU.subtract).then_inc(rest_done, 1)
                    pool.wait_ge(middle_done, s + 1)
                    nc.gpsimd.tensor_tensor(parts[:, slot, :, 2 * D:3 * D], rest[:, slot, :, :], parts[:, slot, :, D:2 * D],
                                            ALU.subtract).then_inc(parts_ready, 1)
                paired_loop(pool, BATCHES, body)

            @block.scalar
            def _(act):
                def body(s, slot):
                    wait(act, parts_free, s * BATCH - BATCH)
                    nc.scalar.activation(parts[:, slot, :, 0:D], messages[:, bass.ds(s * BATCH, BATCH), :], ACT.Copy).then_inc(high_done, 1)
                    act.wait_ge(rest_done, s + 1)
                    nc.scalar.activation(parts[:, slot, :, D:2 * D], rest[:, slot, :, :], ACT.Copy).then_inc(middle_done, 1)
                paired_loop(act, BATCHES, body)

            @block.vector
            def _(dve):
                near_or_far(dve, vector_part)

            @block.tensor
            def _(pe):
                near_or_far(pe, tensor_part)

        sums = sb(ctx, name("sums"), [COLS, NODES], F32)
        value = sb(ctx, name("value"), [128, NODE_TILES, D], F32)
        square = sb(ctx, name("square"), [128, NODE_TILES, D], F32)
        stat = sb(ctx, name("stat"), [128, NODE_TILES], F32)
        count = sb(ctx, name("count"), [128, NODE_TILES], F32)
        root = sb(ctx, name("root"), [128, NODE_TILES], F32)
        sums_copied = sem(name("sums_copied"))
        nodes_summed = sem(name("nodes_summed"))
        variance_done = sem(name("variance_done"))
        root_done = sem(name("root_done"))
        node_step = sem(name("node_step"))
        stored = sem(name("stored"))
        HALF = -(-NODE_TILES // 2)
        node_ps = pb(ctx, name("node_ps"), [128, BANK])

        def node_sums(half):
            n = HALF if half == 0 else NODE_TILES - HALF
            return node_ps[:, 0:n * (D + 1)].rearrange("p (h c) -> p h c", c=D + 1), n

        with ctx, nc.Block() as block:
            @block.scalar
            def _(act):
                for b in range(0, ACC_BANKS, 2):
                    at = slice(b * BANK, min((b + 1) * BANK, NODES))
                    nc.scalar.activation(sums[:, at], sums_ps[:, at], ACT.Copy).then_inc(sums_copied, 1)
                act.wait_ge(variance_done, 1)
                nc.scalar.activation(root[:, :], stat[:, :], ACT.Sqrt).then_inc(root_done, 1)

            @block.tensor
            def _(pe):
                pe.wait_ge(sums_copied, ACC_BANKS)
                for half in range(2):
                    to, n = node_sums(half)
                    if half:
                        pe.wait_ge(node_step, 1)
                    for h in range(n):
                        tile = half * HALF + h
                        last = nc.tensor.matmul(to[:, h, :], sums[:, tile * NODE_TILE:(tile + 1) * NODE_TILE], sum_parts_sb[:, :], start=True, stop=True)
                    last.then_inc(nodes_summed, 1)

            @block.vector
            def _(dve):
                v = nc.vector
                done = [0]

                def step(instruction):
                    done[0] += 1
                    instruction.then_inc(node_step, 1)
                    dve.wait_ge(node_step, done[0])

                for b in range(1, ACC_BANKS, 2):
                    at = slice(b * BANK, min((b + 1) * BANK, NODES))
                    v.tensor_copy(sums[:, at], sums_ps[:, at]).then_inc(sums_copied, 1)
                wide = lambda a: a.unsqueeze(2).to_broadcast([128, NODE_TILES, D])
                for half in range(2):
                    of, n = node_sums(half)
                    at = slice(half * HALF, half * HALF + n)
                    dve.wait_ge(nodes_summed, half + 1)
                    v.tensor_scalar(count[:, at], of[:, :, D], 1.0, None, ALU.max)
                    step(v.tensor_copy(value[:, at, :], of[:, :, 0:D]))
                step(v.reciprocal(count[:, :], count[:, :]))
                step(v.tensor_tensor(value[:, :, :], value[:, :, :], wide(count[:, :]), ALU.mult))
                step(v.tensor_tensor(value[:, :, :], value[:, :, :], b2_sb[:, :].unsqueeze(1).to_broadcast([128, NODE_TILES, D]), ALU.add))
                step(v.tensor_scalar(value[:, :, :], value[:, :, :], 0.0, None, ALU.max))
                step(v.tensor_tensor(value[:, :, :], value[:, :, :], node_feats[:, 0:NODE_TILES, :], ALU.add))
                normalize(dve, step, 1, value, square, stat, root, variance_done, root_done)
                v.sem_inc(sums_done, 1)

            @block.sync
            def _(sp):
                sp.wait_ge(sums_done, 1)
                sp.dma_start(out[0:FULL * NODE_TILE, :].rearrange("(h p) d -> p h d", p=NODE_TILE), node_feats[:, 0:FULL, :]).then_inc(stored, 16)
                sp.dma_start(out[FULL * NODE_TILE:N, :], node_feats[0:TAIL, FULL, :]).then_inc(stored, 16)
                sp.wait_ge(stored, 32)

    message_stage(0)
    source_stage()
    message_stage(1)
    target_stage()
    top.close()


def laid_out(x, src, dst, edge_attr_16, L0_gnn_kernel, L0_gnn_bias, L1_gnn_W1, L1_gnn_b1, L1_gnn_W2, L1_gnn_b2):
    a = {k: np.asarray(v) for k, v in locals().items()}
    x, src, dst, bond = a["x"], a["src"], a["dst"], a["edge_attr_16"]
    D, E, BOND = x.shape[1], src.shape[0], bond.shape[1]
    nodes = -(-x.shape[0] // NODE_TILE) * NODE_TILE
    row = np.arange(BOND * D) // D
    spread_bond = np.tile(np.arange(BOND)[:, None] == row[None, :], (SPLIT, 1)).reshape(SPLIT * BOND, -1, 128)
    spread_x = np.arange(128)[:, None] % D == np.arange(128)[None, :] % D
    column = np.arange(128)
    sum_quarters = (column // (SPLIT * D) * D + column % D)[:, None] == np.arange(2 * D)[None, :]
    sum_parts = np.zeros((PARTS * D + 1, D + 1), np.float32)
    sum_parts[np.arange(PARTS * D), np.arange(PARTS * D) % D] = 1
    sum_parts[PARTS * D, D] = 1
    laid = dict(
        x=x, src_rows=src, dst_rows=dst, src_cols=src.reshape(-1, EDGE_TILE).T, dst_cols=dst.reshape(-1, EDGE_TILE).T,
        bond_rows=bond.T,
        edge_kernel=a["L0_gnn_kernel"].reshape(BOND, D, D).transpose(0, 2, 1).reshape(-1, 128, D).transpose(1, 0, 2),
        edge_bias=a["L0_gnn_bias"].reshape(D, D).T,
        w1_node=a["L1_gnn_W1"].T[:D], w1_edge=a["L1_gnn_W1"].T[D:], b1=a["L1_gnn_b1"][:, None],
        w2=a["L1_gnn_W2"].T, b2=a["L1_gnn_b2"][None, :],
        node_row=np.arange(nodes, dtype=np.int16)[None, :],
        node_col=np.arange(-(-nodes // (HALVES * NODE_TILE)) * NODE_TILE, dtype=np.float32).reshape(-1, NODE_TILE).T,
        tile_starts=np.arange(0, nodes, NODE_TILE, dtype=np.float32)[None, :],
        spread_bond=spread_bond.astype(np.float32), spread_x=spread_x.astype(np.float32),
        sum_quarters=sum_quarters.astype(np.float32), sum_parts=sum_parts, identity=np.eye(128, dtype=np.float32))
    return {k: np.ascontiguousarray(v) for k, v in laid.items()}


def kernel(**inputs):
    import concourse.bacc as bacc
    from concourse.bass_utils import run_bass_kernel_spmd

    arrays = laid_out(**inputs)
    nc = bacc.Bacc("TRN2", target_bir_lowering=False, num_devices=1)
    args = {n: nc.dram_tensor(n, v.shape, mybir.dt.from_np(v.dtype), kind="ExternalInput").ap() for n, v in arrays.items()}
    out = nc.dram_tensor("out", arrays["x"].shape, F32, kind="ExternalOutput").ap()
    gnn_program(nc, **args, out=out)
    r = run_bass_kernel_spmd(nc, [arrays], core_ids=[0])
    return r.results[0]["out"]
```

```python
from contextlib import ExitStack

import concourse.bass as bass
import numpy as np
from concourse import mybir

F32 = mybir.dt.float32
F32R = mybir.dt.float32r
BF16 = mybir.dt.bfloat16
I16 = mybir.dt.int16
I32 = mybir.dt.int32
ALU = mybir.AluOpType
ACT = mybir.ActivationFunctionType
AX = mybir.AxisListType

EDGE_TILE = 125
GROUP_TILES = 4
GROUP = EDGE_TILE * GROUP_TILES
SUPER_GROUPS = 2
SUPER = GROUP * SUPER_GROUPS
NODE_TILE = 128
BANK = 512
SPLIT = 2
PARTS = 3
HALVES = 2
QUARTERS = 4
WINDOW_NODES = NODE_TILE // SPLIT
SPAN = BANK - WINDOW_NODES
BONDS_AT = (48, 64, 0, 96)
EPS = 1e-5


def wait(engine, semaphore, value):
    if not (isinstance(value, int) and value <= 0):
        engine.wait_ge(semaphore, value)


def first_use(s):
    return isinstance(s, int) and s == 0


def times(s, slot):
    return s // 2 + 1 if isinstance(s, int) else (s - slot) // 2 + 1


def paired_loop(engine, count, body):
    body(0, 0)
    body(1, 1)
    with engine.Fori(1, count // 2) as r:
        body(r * 2, 0)
        body(r * 2 + 1, 1)


def gnn_program(nc, x, src_rows, dst_rows, src_cols, dst_cols, bond_rows, edge_kernel, edge_bias, w1_node, w1_edge,
                b1, w2, b2, node_row, node_col, window_col, span_starts, spread_bond, spread_x, sum_quarters, sum_parts, identity, out):
    N, D = x.shape
    E = src_rows.shape[0]
    BOND = bond_rows.shape[0]
    HID = w1_node.shape[1]
    TILES = E // EDGE_TILE
    GROUPS = E // GROUP
    SUPERS = E // SUPER
    NODE_TILES = -(-N // NODE_TILE)
    FULL = N // NODE_TILE
    TAIL = N - FULL * NODE_TILE
    NODES = NODE_TILES * NODE_TILE
    HALF_TILES = -(-NODE_TILES // HALVES)
    HALF_NODES = HALF_TILES * NODE_TILE
    QUARTER_NODES = NODES // QUARTERS
    TABLE_TILES = HALVES * HALF_TILES
    CHUNKS = BOND * D // 128
    REPEAT = 128 // D
    COLS = PARTS * D + 1
    ACC_BANKS = -(-(NODES - WINDOW_NODES) // SPAN)
    ROWS_DST, ROWS_DST_NEAR, ROWS_SRC = range(3)

    top = ExitStack()

    def sb(ctx, name, shape, dt):
        return ctx.enter_context(nc.sbuf_tensor(name, shape, dt))

    def pb(ctx, name, shape, dt=F32):
        return ctx.enter_context(nc.psum_tensor(name, shape, dt))

    def sem(name):
        return top.enter_context(nc.semaphore(name))

    row_table = nc.dram_tensor("row_table", (3, E), I16, kind="Internal").ap()
    half_table = nc.dram_tensor("half_table", (2, HALVES, E), BF16, kind="Internal").ap()
    window_table = nc.dram_tensor("window_table", (TABLE_TILES * NODE_TILE, SPLIT * 128), F32, kind="Internal").ap()
    bond_parts_dram = nc.dram_tensor("bond_parts_dram", (SPLIT * BOND, E), F32, kind="Internal").ap()
    low_dram = nc.dram_tensor("low_dram", (1, GROUPS), F32, kind="Internal").ap()
    first_dram = nc.dram_tensor("first_dram", (2, GROUPS), I32, kind="Internal").ap()
    spread_dram = nc.dram_tensor("spread_dram", (1, GROUPS), F32, kind="Internal").ap()

    node_feats = sb(top, "node_feats", [128, TABLE_TILES, D], F32)
    pair_parts = sb(top, "pair_parts", [128, HALF_TILES, HALVES, SPLIT, D], F32R)
    node_iota = sb(top, "node_iota", [EDGE_TILE, NODES], I16)
    node_id = sb(top, "node_id", [128, HALF_TILES], F32)
    src_quarter_col = sb(top, "src_quarter_col", [EDGE_TILE, TILES], F32)
    src_quarter = sb(top, "src_quarter", [EDGE_TILE, TILES], BF16)
    dst_col = sb(top, "dst_col", [EDGE_TILE, TILES], F32)
    dst_near_col = sb(top, "dst_near_col", [EDGE_TILE, TILES], F32)
    first = sb(top, "first", [1, 2, GROUPS], I32)
    is_near = sb(top, "is_near", [1, 1], I32)
    kernel_sb = sb(top, "kernel_sb", [128, CHUNKS, D], F32)
    bias_sb = sb(top, "bias_sb", [128, D], F32)
    w1_node_parts = sb(top, "w1_node_parts", [128, SPLIT, 128], F32R)
    w1_edge_parts = sb(top, "w1_edge_parts", [128, 128], F32R)
    window_id = sb(top, "window_id", [128, 1], F32)
    b1_sb = sb(top, "b1_sb", [HID, 1], F32)
    w2_sb = sb(top, "w2_sb", [128, D], F32)
    b2_sb = sb(top, "b2_sb", [128, D], F32)
    spread_bond_sb = sb(top, "spread_bond_sb", [128, CHUNKS, 128], F32R)
    spread_x_sb = sb(top, "spread_x_sb", [128, 128], F32R)
    sum_quarters_sb = sb(top, "sum_quarters_sb", [128, 2 * D], F32)
    sum_parts_sb = sb(top, "sum_parts_sb", [COLS, D + 1], F32)
    identity_sb = sb(top, "identity_sb", [128, 128], F32)
    zeros = sb(top, "zeros", [128, BANK], BF16)

    def pair_views(half):
        return pair_parts[:, :, half, 0, :], pair_parts[:, :, half, 1, :], node_feats[:, half * HALF_TILES:(half + 1) * HALF_TILES, :]

    def make_pairs(step, vec):
        for half in range(HALVES):
            high, low, whole = pair_views(half)
            step(vec.tensor_copy(high, whole))
            step(vec.tensor_tensor(low, whole, high, ALU.subtract))

    with ExitStack() as ctx:
        PREP = GROUPS // 2
        PER = GROUPS // PREP
        rows_i = sb(ctx, "rows_i", [PREP, 2, PER * GROUP], I32)
        rows_f = sb(ctx, "rows_f", [PREP, 2, PER * GROUP], F32)
        half_f = sb(ctx, "half_f", [PREP, 2, PER * GROUP], F32)
        pick_16 = sb(ctx, "pick_16", [PREP, 2, PER * GROUP], I16)
        near_16 = sb(ctx, "near_16", [PREP, PER * GROUP], I16)
        halves = sb(ctx, "halves", [PREP, 2, HALVES, PER * GROUP], BF16)
        low = sb(ctx, "low", [PREP, PER], F32)
        high = sb(ctx, "high", [PREP, PER], F32)
        bank = sb(ctx, "bank", [PREP, PER], F32)
        column = sb(ctx, "column", [PREP, PER], F32)
        first_i = sb(ctx, "first_i", [PREP, 2, PER], I32)
        spread = sb(ctx, "spread", [PREP, PER], F32)
        at_least = sb(ctx, "at_least", [PREP, ACC_BANKS - 1], F32)
        starts = sb(ctx, "starts", [PREP, ACC_BANKS - 1], F32)
        col_i = sb(ctx, "col_i", [EDGE_TILE, 2, TILES], I32)
        col_f = sb(ctx, "col_f", [EDGE_TILE, TILES], F32)
        quarter = sb(ctx, "quarter", [EDGE_TILE, TILES], F32)
        above = sb(ctx, "above", [EDGE_TILE, TILES], F32)
        low_wide = sb(ctx, "low_wide", [EDGE_TILE, GROUPS], F32)
        spread_row = sb(ctx, "spread_row", [1, GROUPS], F32)
        widest = sb(ctx, "widest", [1, 1], F32)
        x_wide = sb(ctx, "x_wide", [128, TABLE_TILES, SPLIT, REPEAT, D], F32R)
        w_node_f = sb(ctx, "w_node_f", [128, 2, HID], F32)
        w_edge_f = sb(ctx, "w_edge_f", [128, HID], F32)
        w_edge_high = sb(ctx, "w_edge_high", [128, HID], F32R)
        spread_bond_f = sb(ctx, "spread_bond_f", [128, CHUNKS, 128], F32)
        spread_x_f = sb(ctx, "spread_x_f", [128, 128], F32)

        cleared = sem("cleared")
        rows_loaded = sem("rows_loaded")
        cols_loaded = sem("cols_loaded")
        nodes_loaded = sem("nodes_loaded")
        consts_loaded = sem("consts_loaded")
        tiles_known = sem("tiles_known")
        rows_ready = sem("rows_ready")
        wide_ready = sem("wide_ready")
        halves_known = sem("halves_known")
        halves_ready = sem("halves_ready")
        wide_high = sem("wide_high")
        pairs_high = sem("pairs_high")
        consts_high = sem("consts_high")
        prep_stored = sem("prep_stored")
        rows_stored = sem("rows_stored")
        wide_stored = sem("wide_stored")
        near_loaded = sem("near_loaded")
        prep_step = sem("prep_step")

        wide = node_feats[:, :, :].unsqueeze(2).to_broadcast([128, TABLE_TILES, REPEAT, D])
        by_prep = lambda row: row.rearrange("(q c) -> q c", q=PREP)
        consts = [(node_iota[:, :], node_row.partition_broadcast(EDGE_TILE)), (node_id[:, :], node_col),
                  (kernel_sb[:, :, :], edge_kernel), (bias_sb[0:D, :], edge_bias), (b1_sb[:, :], b1),
                  (w2_sb[0:HID, :], w2), (b2_sb[:, :], b2.partition_broadcast(128)),
                  (window_id[:, :], window_col), (spread_x_f[:, :], spread_x),
                  (sum_quarters_sb[:, :], sum_quarters), (sum_parts_sb[:, :], sum_parts), (identity_sb[:, :], identity)]
        consts += [(w_node_f[i * D:(i + 1) * D, 0, :], w1_node) for i in range(128 // D)]
        consts += [(w_edge_f[at:at + BOND, :], w1_edge) for at in BONDS_AT]
        consts += [(spread_bond_f[at:at + BOND, :, :], spread_bond) for at in BONDS_AT[:SPLIT]]

        with nc.Block() as block:
            @block.sync
            def _(sp):
                sp.dma_start(rows_i[:, 0, :], by_prep(dst_rows)).then_inc(rows_loaded, 16)
                sp.dma_start(rows_i[:, 1, :], by_prep(src_rows)).then_inc(rows_loaded, 16)
                sp.dma_start(starts[:, :], span_starts.partition_broadcast(PREP)).then_inc(rows_loaded, 16)
                sp.wait_ge(cleared, 1)
                sp.dma_start(node_feats[:, 0:FULL, :], x[0:FULL * NODE_TILE, :].rearrange("(h p) d -> p h d", p=NODE_TILE)).then_inc(nodes_loaded, 16)
                sp.dma_start(node_feats[0:TAIL, FULL, :], x[FULL * NODE_TILE:N, :]).then_inc(nodes_loaded, 16)
                sp.dma_start(col_i[:, 0, :], src_cols).then_inc(cols_loaded, 16)
                sp.dma_start(col_i[:, 1, :], dst_cols).then_inc(cols_loaded, 16)
                for to, of in consts[:len(consts) // 2]:
                    sp.dma_start(to, of).then_inc(consts_loaded, 16)
                sp.wait_ge(wide_ready, 1)
                sp.dma_start(window_table.rearrange("(h p) c -> p h c", p=NODE_TILE),
                             x_wide[:, :, :, :, :].rearrange("p h s r d -> p h (s r d)").bitcast(F32)).then_inc(wide_stored, 16)
                for to, of in consts[len(consts) // 2:]:
                    sp.dma_start(to, of).then_inc(consts_loaded, 16)
                sp.wait_ge(wide_stored, 16)

            @block.gpsimd
            def _(pool):
                for t in (node_feats[:, FULL:TABLE_TILES, :], bias_sb[:, :], w2_sb[:, :], spread_bond_f[:, :, :], w_edge_f[:, :],
                          w1_node_parts[:, :, :].bitcast(F32), w1_edge_parts[:, :].bitcast(F32), zeros[:, :]):
                    last = nc.gpsimd.memset(t, 0.0)
                last.then_inc(cleared, 1)

            @block.scalar
            def _(act):
                def stores():
                    act.wait_ge(nodes_loaded, 32)
                    nc.scalar.activation(x_wide[:, :, 0, :, :], wide, ACT.Copy).then_inc(wide_high, 1)
                    act.wait_ge(tiles_known, 1)
                    act.dma_start(low_dram.rearrange("o (q c) -> (o q) c", q=PREP), low[:, :]).then_inc(prep_stored, 16)
                    act.dma_start(first_dram.rearrange("o (q c) -> q o c", q=PREP), first_i[:, :, :]).then_inc(prep_stored, 16)
                    act.dma_start(spread_dram.rearrange("o (q c) -> (o q) c", q=PREP), spread[:, :]).then_inc(prep_stored, 16)
                    act.wait_ge(prep_stored, 48)
                    act.dma_start(low_wide[:, :], low_dram.partition_broadcast(EDGE_TILE)).then_inc(near_loaded, 16)
                    act.dma_start(first[:, :, :], first_dram.unsqueeze(0)).then_inc(near_loaded, 16)
                    act.dma_start(spread_row[:, :], spread_dram).then_inc(near_loaded, 16)
                    act.wait_ge(halves_known, 1)
                    nc.scalar.activation(halves[:, :, 1, :], half_f[:, :, :], ACT.Copy).then_inc(halves_ready, 1)
                    nc.scalar.activation(halves[:, :, 0, :], half_f[:, :, :], ACT.Relu, bias=1.0, scale=-1.0).then_inc(halves_ready, 1)
                    act.wait_ge(rows_ready, 1)
                    act.wait_ge(halves_ready, 2)
                    act.dma_start(by_prep(row_table[ROWS_DST, :]), pick_16[:, 0, :]).then_inc(rows_stored, 16)
                    act.dma_start(by_prep(row_table[ROWS_DST_NEAR, :]), near_16[:, :]).then_inc(rows_stored, 16)
                    act.dma_start(by_prep(row_table[ROWS_SRC, :]), pick_16[:, 1, :]).then_inc(rows_stored, 16)
                    for side in range(2):
                        for half in range(HALVES):
                            act.dma_start(by_prep(half_table[side, half, :]), halves[:, side, half, :]).then_inc(rows_stored, 16)

                stores()
                for half in range(HALVES):
                    high_part, _, whole = pair_views(half)
                    nc.scalar.activation(high_part, whole, ACT.Copy).then_inc(pairs_high, 1)
                act.wait_ge(consts_loaded, 16 * len(consts))
                for to, of in ((spread_bond_sb[:, :, :], spread_bond_f[:, :, :]), (spread_x_sb[:, :], spread_x_f[:, :]),
                               (w1_node_parts[:, 0, 0:HID], w_node_f[:, 0, :]), (w_edge_high[:, :], w_edge_f[:, :])):
                    nc.scalar.activation(to, of, ACT.Copy).then_inc(consts_high, 1)
                act.wait_ge(rows_stored, 16 * (3 + 2 * HALVES))

            @block.vector
            def _(dve):
                done = [0]

                def step(instruction):
                    done[0] += 1
                    instruction.then_inc(prep_step, 1)
                    dve.wait_ge(prep_step, done[0])

                v = nc.vector

                dve.wait_ge(rows_loaded, 48)
                step(v.tensor_copy(rows_f[:, :, :], rows_i[:, :, :]))
                groups = rows_f[:, 0, :].rearrange("q (g e) -> q g e", g=PER)
                step(v.tensor_reduce(low[:, :], groups, AX.X, ALU.min))
                step(v.tensor_reduce(high[:, :], groups, AX.X, ALU.max))
                for g in range(PER):
                    step(v.tensor_scalar(at_least[:, :], starts[:, :], low[:, g:g + 1], None, ALU.is_le, ALU.add, accum_out=bank[:, g:g + 1]))
                step(v.tensor_tensor(spread[:, :], high[:, :], low[:, :], ALU.subtract))
                step(v.scalar_tensor_tensor(out=column[:, :], in0=bank[:, :], scalar=float(WINDOW_NODES), in1=low[:, :], op0=ALU.mult, op1=ALU.add))
                step(v.tensor_copy(first_i[:, 0, :], column[:, :]))
                step(v.tensor_copy(first_i[:, 1, :], low[:, :]))
                v.sem_inc(tiles_known, 1)
                dve.wait_ge(wide_high, 1)
                step(v.tensor_tensor(x_wide[:, :, 1, :, :], wide, x_wide[:, :, 0, :, :], ALU.subtract))
                v.sem_inc(wide_ready, 1)
                step(v.tensor_scalar(half_f[:, :, :], rows_f[:, :, :], float(HALF_NODES), None, ALU.is_ge))
                v.sem_inc(halves_known, 1)
                step(v.scalar_tensor_tensor(out=pick_16[:, :, :], in0=half_f[:, :, :], scalar=-float(HALF_NODES), in1=rows_f[:, :, :],
                                            op0=ALU.mult, op1=ALU.add))
                for g in range(PER):
                    at = slice(g * GROUP, (g + 1) * GROUP)
                    step(v.tensor_scalar(near_16[:, at], rows_f[:, 0, at], low[:, g:g + 1], None, ALU.subtract))
                v.sem_inc(rows_ready, 1)
                dve.wait_ge(cols_loaded, 32)
                step(v.tensor_copy(col_f[:, :], col_i[:, 0, :]))
                step(v.tensor_scalar(quarter[:, :], col_f[:, :], float(QUARTER_NODES), None, ALU.is_ge))
                for q in range(2, QUARTERS):
                    step(v.tensor_scalar(above[:, :], col_f[:, :], float(q * QUARTER_NODES), None, ALU.is_ge))
                    step(v.tensor_tensor(quarter[:, :], quarter[:, :], above[:, :], ALU.add))
                step(v.scalar_tensor_tensor(out=src_quarter_col[:, :], in0=quarter[:, :], scalar=-float(QUARTER_NODES), in1=col_f[:, :],
                                            op0=ALU.mult, op1=ALU.add))
                step(v.tensor_copy(src_quarter[:, :], quarter[:, :]))
                step(v.tensor_copy(dst_col[:, :], col_i[:, 1, :]))
                dve.wait_ge(near_loaded, 48)
                step(v.tensor_tensor(dst_near_col[:, :].rearrange("p (g t) -> p g t", g=GROUPS),
                                     dst_col[:, :].rearrange("p (g t) -> p g t", g=GROUPS),
                                     low_wide[:, :].unsqueeze(2).to_broadcast([EDGE_TILE, GROUPS, GROUP_TILES]), ALU.subtract))
                step(v.tensor_reduce(widest[:, :], spread_row[:, :], AX.X, ALU.max))
                step(v.tensor_scalar(is_near[:, :], widest[:, :], float(WINDOW_NODES - 1), None, ALU.is_le))
                dve.wait_ge(pairs_high, HALVES)
                for half in range(HALVES):
                    high_part, low_part, whole = pair_views(half)
                    step(v.tensor_tensor(low_part, whole, high_part, ALU.subtract))
                dve.wait_ge(consts_high, 4)
                step(v.tensor_tensor(w1_node_parts[:, 1, 0:HID], w_node_f[:, 0, :], w1_node_parts[:, 0, 0:HID], ALU.subtract))
                for i, at in enumerate(BONDS_AT):
                    rows = slice(at // 32 * 32, at // 32 * 32 + 32)
                    if i < SPLIT:
                        step(v.tensor_copy(w1_edge_parts[rows, 0:HID], w_edge_high[rows, :]))
                    else:
                        step(v.tensor_tensor(w1_edge_parts[rows, 0:HID], w_edge_f[rows, :], w_edge_high[rows, :], ALU.subtract))

    messages = sb(top, "messages", [EDGE_TILE, TILES, D], F32)

    def message_stage(layer):
        ctx = ExitStack()
        name = lambda n: f"{n}_m{layer}"
        ACT_PICKS = (4, 8, 12) if layer else ()
        POOL_PICKS = () if layer else (0,)
        VECTOR_PICKS = [h for h in range(HALF_TILES) if h not in ACT_PICKS + POOL_PICKS]
        RING = 5 if layer else 3
        BANKS = 2 if layer else 1
        index = sb(ctx, name("index"), [128, 2, SUPER], I16)
        mask = sb(ctx, name("mask"), [128, 2, SUPER], BF16)
        bond = sb(ctx, name("bond"), [128, 2, SUPER], F32R)
        pick = sb(ctx, name("pick"), [128, RING + len(ACT_PICKS) + len(POOL_PICKS), SUPER], F32R)
        gathered = sb(ctx, name("gathered"), [128, 2, SUPER], F32R)
        turned = sb(ctx, name("turned"), [128, 2, SUPER_GROUPS, EDGE_TILE], F32)
        gather_ps = pb(ctx, name("gather_ps"), [128, BANKS * SUPER_GROUPS, BANK])
        turned_ps = pb(ctx, name("turned_ps"), [128, BANK])
        send_ps = pb(ctx, name("send_ps"), [EDGE_TILE, BANK])

        index_loaded = [sem(name(f"index_loaded{i}")) for i in range(2)]
        mask_loaded = [sem(name(f"mask_loaded{i}")) for i in range(2)]
        bond_loaded = [sem(name(f"bond_loaded{i}")) for i in range(2)]
        bond_cleared = sem(name("bond_cleared"))
        bond_high = sem(name("bond_high"))
        bond_split = sem(name("bond_split"))
        slot_free = sem(name("slot_free"))
        COPIES = 3 if layer else SPLIT
        CLEARS = 1 if layer else SUPER_GROUPS
        first_ready = sem(name("first_ready"))
        act_ready = sem(name("act_ready"))
        first_free = sem(name("first_free"))
        pick_ready = sem(name("pick_ready"))
        pick_used = sem(name("pick_used"))
        raw_ready = sem(name("raw_ready"))
        gather_ready = sem(name("gather_ready"))
        TURNS = 1 if layer else 2
        turned_done = sem(name("turned_done"))
        turned_copied = sem(name("turned_copied"))
        send_done = sem(name("send_done"))
        send_copied = sem(name("send_copied"))
        if layer == 0:
            window = gathered[:, :, :].rearrange("p a e -> p (a e)")[:, 0:2 * SUPER_GROUPS * 128].rearrange("p (g c) -> p g c", c=128)
            x_sb = sb(ctx, name("x_sb"), [128, 2, GROUP], F32)
            outer = sb(ctx, name("outer"), [128, 2, CHUNKS, GROUP], F32)
            bond_ps = pb(ctx, name("bond_ps"), [128, CHUNKS, BANK])
            window_rows = window_table.rearrange("n (s c) -> (n s) c", s=SPLIT)
            window_loaded = [sem(name(f"window_loaded{i}")) for i in range(2 * SUPER_GROUPS)]
            x_spread = sem(name("x_spread"))
            x_copied = sem(name("x_copied"))
            bond_spread = sem(name("bond_spread"))
            outer_done = sem(name("outer_done"))
            bias_done = sem(name("bias_done"))
            bond_whole = sb(ctx, name("bond_whole"), [128, 2, SUPER], F32)
            raw = sb(ctx, name("raw"), [128, SUPER], F32)
            bond_stored = [sem(name(f"bond_stored{i}")) for i in range(2)]
            features_used = x_spread
        else:
            hidden = sb(ctx, name("hidden"), [128, 2, GROUP], F32)
            less_id = sb(ctx, name("less_id"), [128, HALF_TILES], F32)
            distance_ready = sem(name("distance_ready"))
            id_ready = sem(name("id_ready"))
            hidden_ps = pb(ctx, name("hidden_ps"), [128, 2, BANK])
            hidden_cleared = sem(name("hidden_cleared"))
            hidden_done = sem(name("hidden_done"))
            relu_done = sem(name("relu_done"))
            features_used = hidden_done

        SUPER_TILES = SUPER_GROUPS * GROUP_TILES

        def by_group(ps):
            return ps[:, 0:SUPER_GROUPS * EDGE_TILE].rearrange("p (k e) -> p k e", e=EDGE_TILE)

        def pick_slot(h):
            return VECTOR_PICKS.index(h) % RING if h in VECTOR_PICKS else RING + (ACT_PICKS + POOL_PICKS).index(h)

        def pick_before(s, h):
            slot = pick_slot(h)
            earlier = [g for g in range(h) if pick_slot(g) == slot]
            if earlier:
                return s * HALF_TILES + earlier[-1] + 1
            return s * HALF_TILES - HALF_TILES + max(g for g in range(HALF_TILES) if pick_slot(g) == slot) + 1

        def sync_part(sp, near):
            row = ROWS_SRC if layer else ROWS_DST_NEAR if near else ROWS_DST
            H = 1 if near else len(VECTOR_PICKS)

            def body(s, slot):
                start = s * SUPER if isinstance(s, int) else sp.snap(s * SUPER)
                before = start - 2 * SUPER if isinstance(s, int) else sp.snap(s * SUPER - 2 * SUPER)
                if near:
                    lowest = [sp.value_load(first[0:1, 1, bass.ds(s * SUPER_GROUPS + k, 1)], min_val=0, max_val=TABLE_TILES * NODE_TILE - WINDOW_NODES)
                              for k in range(SUPER_GROUPS)]
                wait(sp, pick_ready, s * H - H)
                if layer == 1:
                    sp.sem_inc(slot_free, 1)
                    wait(sp, act_ready, s * len(ACT_PICKS) - len(ACT_PICKS))
                elif not near:
                    sp.sem_inc(slot_free, 1)
                    wait(sp, first_ready, s - 1)
                sp.sem_inc(slot_free, 1)
                sp.dma_start(index[:, slot, :], row_table[row:row + 1, bass.ds(start, SUPER)].partition_broadcast(128)).then_inc(index_loaded[slot], 16)
                def load_bonds():
                    if first_use(s):
                        sp.wait_ge(bond_cleared, 1)
                    elif layer == 1:
                        wait(sp, hidden_done, s * SUPER_GROUPS - SUPER_GROUPS)
                    elif not (isinstance(s, int) and s < 2):
                        store_bonds(s, slot, before)
                    sp.sem_inc(slot_free, 1)
                    if layer == 0:
                        for at in BONDS_AT[:SPLIT]:
                            sp.dma_start(bond_whole[at:at + BOND, slot, :], bond_rows[:, bass.ds(start, SUPER)]).then_inc(bond_loaded[slot], 16)
                    else:
                        for at, of in ((BONDS_AT[0], bond_parts_dram), (BONDS_AT[2], bond_parts_dram[0:BOND, :]), (BONDS_AT[3], bond_parts_dram[BOND:, :])):
                            sp.dma_start(bond[at:at + of.shape[0], slot, :].bitcast(F32), of[:, bass.ds(start, SUPER)]).then_inc(bond_loaded[slot], 16)

                if layer == 0:
                    load_bonds()
                if near:
                    wait(sp, x_spread, s * SUPER_GROUPS - SUPER_GROUPS)
                    sp.sem_inc(slot_free, 1)
                    for k in range(SUPER_GROUPS):
                        at = slot * SUPER_GROUPS + k
                        sp.dma_start(window[:, at, :].bitcast(F32), window_rows[bass.ds(lowest[k] * SPLIT, 128), :]).then_inc(window_loaded[at], 16)
                else:
                    wait(sp, gather_ready, s * CLEARS - CLEARS)
                    sp.sem_inc(slot_free, 1)
                    for half in range(HALVES):
                        sp.dma_start(mask[half * 64:half * 64 + 64, slot, :],
                                     half_table[layer, half:half + 1, bass.ds(start, SUPER)].partition_broadcast(64)).then_inc(mask_loaded[slot], 16)
                if layer == 1:
                    load_bonds()

            def store_bonds(s, slot, start):
                sp.wait_ge(bond_split, s - 1)
                sp.sem_inc(slot_free, 1)
                at = BONDS_AT[0]
                sp.dma_start(bond_parts_dram[:, bass.ds(start, SUPER)], bond[at:at + SPLIT * BOND, slot, :].bitcast(F32)).then_inc(bond_stored[slot], 16)

            paired_loop(sp, SUPERS, body)
            if layer == 0:
                for slot in range(2):
                    store_bonds(SUPERS + slot, slot, (SUPERS - 2 + slot) * SUPER)
                for slot in range(2):
                    sp.wait_ge(bond_stored[slot], 16 * (SUPERS // 2))

        def vector_part(dve, near):
            def clear_half(s, slot):
                dve.wait_ge(pick_used, s * HALF_TILES + HALF_TILES)
                dve.wait_ge(mask_loaded[slot], times(s, slot) * 16 * HALVES)
                wait(dve, hidden_done, s * SUPER_GROUPS - SUPER_GROUPS)
                banks = slice(slot * SUPER_GROUPS, (slot + 1) * SUPER_GROUPS)
                nc.vector.tensor_tensor(gathered[:, slot, :].rearrange("p (k e) -> p k e", e=GROUP), gather_ps[:, banks, 0:GROUP],
                                        mask[:, slot, :].rearrange("p (k e) -> p k e", e=GROUP), ALU.mult).then_inc(gather_ready, 1)

            def picks(s, slot):
                dve.wait_ge(index_loaded[slot], times(s, slot) * 16)
                for h in range(1) if near else VECTOR_PICKS:
                    if layer == 1 and VECTOR_PICKS.index(h) == RING and not first_use(s):
                        clear_half(s - 1, 1 - slot)
                    if near:
                        wait(dve, x_spread, s * SUPER_GROUPS - SUPER_GROUPS)
                    else:
                        wait(dve, pick_used, pick_before(s, h))
                    nc.vector.tensor_scalar(pick[:, slot if near else pick_slot(h), :], index[:, slot, :], window_id[:, 0:1] if near else node_id[:, h:h + 1],
                                            None, ALU.is_equal).then_inc(pick_ready, 1)

            def group(i, k, s, slot):
                for j in range(2):
                    dve.wait_ge(bond_spread, i * 2 + j + 1)
                    dve.wait_ge(x_copied, i + 1)
                    wait(dve, turned_done, (s - 1) * TURNS + j + 1)
                    nc.vector.tensor_tensor(outer[:, k, 2 * j:2 * j + 2, :], bond_ps[:, 2 * j:2 * j + 2, 0:GROUP],
                                            x_sb[:, k:k + 1, :].to_broadcast([128, 2, GROUP]), ALU.mult).then_inc(outer_done, 1)

            def body(s, slot):
                if layer == 0 and not near and not first_use(s):
                    groups(s - 1, 1 - slot)
                picks(s, slot)
                if layer == 0 and near and not first_use(s):
                    groups(s - 1, 1 - slot)

            def groups(s, slot):
                for k in range(SUPER_GROUPS):
                    group(s * 2 + k, k, s, slot)

            paired_loop(dve, SUPERS, body)
            if layer == 0:
                groups(SUPERS - 1, 1)
            else:
                clear_half(SUPERS - 1, 1)

        def scalar_part(act, near):
            H = 1 if near else HALF_TILES

            def evacuate(s, slot):
                if near or layer == 1:
                    return
                act.wait_ge(pick_used, s * H + H)
                wait(act, gather_ready, s * SUPER_GROUPS)
                for k in range(SUPER_GROUPS):
                    nc.scalar.activation(raw[:, k * GROUP:(k + 1) * GROUP], gather_ps[:, k, 0:GROUP], ACT.Copy).then_inc(raw_ready, 1)

            def copy_turned(s, slot):
                act.wait_ge(turned_done, s * TURNS + TURNS)
                nc.scalar.activation(turned[:, slot, :, :], by_group(turned_ps), ACT.Copy).then_inc(turned_copied, 1)

            def copy_sent(s):
                act.wait_ge(send_done, s + 1)
                nc.scalar.activation(messages[:, bass.ds(s * SUPER_TILES, SUPER_TILES), :],
                                     send_ps[:, 0:SUPER_TILES * D].rearrange("p (t d) -> p t d", d=D), ACT.Copy).then_inc(send_copied, 1)

            def bond_parts(s, slot):
                act.wait_ge(bond_loaded[slot], times(s, slot) * 16 * COPIES)
                wait(act, bond_spread, s * (2 * SUPER_GROUPS) - 2 * SUPER_GROUPS)
                wait(act, bond_stored[slot], times(s, slot) * 16 - 16)
                nc.scalar.activation(bond[:, slot, :], bond_whole[:, slot, :], ACT.Copy).then_inc(bond_high, 1)

            def pick_distance(s, slot, n):
                h = ACT_PICKS[n]
                act.wait_ge(index_loaded[slot], times(s, slot) * 16)
                wait(act, pick_used, pick_before(s, h))
                nc.scalar.activation(pick[:, pick_slot(h), :], index[:, slot, :], ACT.Abs, bias=less_id[:, h:h + 1]).then_inc(distance_ready, 1)

            def pick_end(s, n):
                made = pick[:, pick_slot(ACT_PICKS[n]), :]
                act.wait_ge(distance_ready, s * len(ACT_PICKS) + n + 1)
                nc.scalar.activation(made, made, ACT.Relu, bias=1.0, scale=-1.0).then_inc(act_ready, 1)

            def relu(i, k, s):
                act.wait_ge(hidden_done, i + 1)
                wait(act, turned_done, s)
                nc.scalar.activation(hidden[0:HID, k, :], hidden_ps[0:HID, k, 0:GROUP], ACT.Relu, bias=b1_sb[:, 0:1]).then_inc(relu_done, 1)

            def finish(s, slot, more=None):
                copy_x(s * 2, 0, s)
                if more:
                    more()
                if not first_use(s):
                    copy_turned(s - 1, 1 - slot)
                copy_x(s * 2 + 1, 1, s)
                if not first_use(s):
                    copy_sent(s - 1)

            def body(s, slot):
                if layer == 1:
                    pick_distance(s, slot, 0)
                    pick_end(s, 0)
                    pick_distance(s, slot, 1)
                    if not (isinstance(s, int) and s < 2):
                        copy_sent(s - 2)
                    pick_distance(s, slot, 2)
                    pick_end(s, 1)
                    if not first_use(s):
                        relu(s * 2 - 2, 0, s - 1)
                        relu(s * 2 - 1, 1, s - 1)
                    pick_end(s, 2)
                    if not first_use(s):
                        copy_turned(s - 1, 1 - slot)
                    return
                if first_use(s):
                    bond_parts(s, slot)
                else:
                    finish(s - 1, 1 - slot, lambda: bond_parts(s, slot))
                evacuate(s, slot)

            def copy_x(i, k, s):
                act.wait_ge(x_spread, i + 1)
                wait(act, bias_done, s)
                wait(act, outer_done, i * 2 - 2)
                nc.scalar.activation(x_sb[:, k, :], gather_ps[:, k, 0:GROUP], ACT.Copy).then_inc(x_copied, 1)

            paired_loop(act, SUPERS, body)
            if layer == 0:
                finish(SUPERS - 1, 1)
            else:
                copy_sent(SUPERS - 2)
                relu(GROUPS - 2, 0, SUPERS - 1)
                relu(GROUPS - 1, 1, SUPERS - 1)
            copy_turned(SUPERS - 1, 1)
            copy_sent(SUPERS - 1)

        def tensor_part(pe, near):
            H = 1 if near else HALF_TILES

            def gather(s, slot):
                if near:
                    return
                if BANKS == 2:
                    wait(pe, gather_ready, s - 1)
                else:
                    wait(pe, x_copied, s * SUPER_GROUPS)
                for h in range(H):
                    if h in VECTOR_PICKS:
                        pe.wait_ge(pick_ready, s * len(VECTOR_PICKS) + VECTOR_PICKS.index(h) + 1)
                    elif h in ACT_PICKS:
                        pe.wait_ge(act_ready, s * len(ACT_PICKS) + ACT_PICKS.index(h) + 1)
                    else:
                        pe.wait_ge(first_ready, s + 1)
                    for k in range(SUPER_GROUPS):
                        to = slot * SUPER_GROUPS + k if BANKS == 2 else k
                        last = nc.tensor.matmul(gather_ps[:, to, 0:GROUP], pair_parts[:, h, :, :, :].rearrange("p a s d -> p (a s d)"),
                                                pick[:, pick_slot(h), k * GROUP:(k + 1) * GROUP], start=h == 0, stop=h == H - 1)
                    last.then_inc(pick_used, 1)
                    if layer == 1 and not first_use(s):
                        finish(s - 1, 1 - slot, h)

            def turn(left, right, start, stop):
                for t in range(GROUP_TILES):
                    last = nc.tensor.matmul(by_group(turned_ps)[t * D:(t + 1) * D, :, :], left, right[:, :, t * EDGE_TILE:(t + 1) * EDGE_TILE],
                                            start=start, stop=stop, skip_group_check=True)
                return last

            def turn_bias(s):
                wait(pe, turned_copied, s)
                pe.wait_ge(x_copied, s * 2 + 2)
                turn(bias_sb[:, :], x_sb[:, :, :], True, False).then_inc(bias_done, 1)

            def turn_outer(s, j):
                pe.wait_ge(outer_done, s * 4 + j + 3)
                turn(kernel_sb[:, 2 * j, :], outer[:, :, 2 * j, :], False, False)
                turn(kernel_sb[:, 2 * j + 1, :], outer[:, :, 2 * j + 1, :], False, j == 1).then_inc(turned_done, 1)

            def turn_hidden(s):
                pe.wait_ge(relu_done, s * 2 + 2)
                wait(pe, turned_copied, s)
                turn(w2_sb[:, :], hidden[:, :, :], True, True).then_inc(turned_done, 1)

            def send(s, slot):
                pe.wait_ge(turned_copied, s + 1)
                wait(pe, send_copied, s)
                for k in range(SUPER_GROUPS):
                    last = nc.tensor.transpose(send_ps[:, k * 128:(k + 1) * 128], turned[:, slot, k, :], identity_sb[:, :])
                last.then_inc(send_done, 1)

            def hide(i, k, s, slot):
                here = slice(k * GROUP, (k + 1) * GROUP)
                wait(pe, relu_done, i - 1)
                pe.wait_ge(bond_loaded[slot], times(s, slot) * 16 * COPIES)
                nc.tensor.matmul(hidden_ps[:, k, 0:GROUP], w1_edge_parts[:, :], bond[:, slot, here], start=True, stop=False)
                pe.wait_ge(gather_ready, s + 1)
                for part in range(SPLIT):
                    last = nc.tensor.matmul(hidden_ps[:, k, 0:GROUP], w1_node_parts[:, part, :], gathered[:, slot, here],
                                            start=False, stop=part == SPLIT - 1)
                last.then_inc(hidden_done, 1)

            def finish(s, slot, h):
                i = s * 2
                if h == 5:
                    hide(i, 0, s, slot)
                elif h == 6:
                    hide(i + 1, 1, s, slot)
                elif h == 9:
                    turn_hidden(s)
                elif h == 1 and not first_use(s):
                    send(s - 1, 1 - slot)

            def group(i, k, s, slot):
                here = slice(k * GROUP, (k + 1) * GROUP)
                if near:
                    at = slot * SUPER_GROUPS + k
                    pe.wait_ge(window_loaded[at], times(s, slot) * 16)
                    pe.wait_ge(pick_ready, s + 1)
                    wait(pe, x_copied, i - 1)
                    last = nc.tensor.matmul(gather_ps[:, k, 0:GROUP], window[:, at, :], pick[:, slot, here], start=True, stop=True)
                else:
                    pe.wait_ge(gather_ready, i + 1)
                    last = nc.tensor.matmul(gather_ps[:, k, 0:GROUP], spread_x_sb[:, :], gathered[:, slot, here], start=True, stop=True)
                last.then_inc(x_spread, 1)
                pe.wait_ge(bond_split, s + 1)
                for j in range(2):
                    if k == 1 and j == 1:
                        turn_bias(s)
                    wait(pe, outer_done, i * 2 + j - 1)
                    for c in (2 * j, 2 * j + 1):
                        last = nc.tensor.matmul(bond_ps[:, c, 0:GROUP], spread_bond_sb[:, c, :], bond[:, slot, here], start=True, stop=True)
                    last.then_inc(bond_spread, 1)
                    if not first_use(s):
                        if k == 0:
                            turn_outer(s - 1, j)
                        elif j == 0:
                            send(s - 1, 1 - slot)

            if layer == 1:
                pe.wait_ge(hidden_cleared, 1)
                paired_loop(pe, SUPERS, gather)
                for h in range(H):
                    finish(SUPERS - 1, 1, h)
                send(SUPERS - 1, 1)
                return

            def body(s, slot):
                gather(s, slot)
                for k in range(SUPER_GROUPS):
                    group(s * 2 + k, k, s, slot)

            paired_loop(pe, SUPERS, body)
            turn_outer(SUPERS - 1, 0)
            turn_outer(SUPERS - 1, 1)
            send(SUPERS - 1, 1)

        def pool_part(pool, near):
            def first_pick(s, slot):
                pool.wait_ge(index_loaded[slot], times(s, slot) * 16)
                wait(pool, pick_used, pick_before(s, 0))
                pool.sem_inc(first_free, 1)
                nc.gpsimd.tensor_scalar(pick[:, pick_slot(0), :], index[:, slot, :], node_id[:, 0:1], None, ALU.is_equal).then_inc(first_ready, 1)

            def clear_half(s, slot):
                pool.wait_ge(mask_loaded[slot], times(s, slot) * 16 * HALVES)
                wait(pool, features_used, s * SUPER_GROUPS - SUPER_GROUPS)
                for k in range(SUPER_GROUPS):
                    here = slice(k * GROUP, (k + 1) * GROUP)
                    pool.wait_ge(raw_ready, s * SUPER_GROUPS + k + 1)
                    nc.gpsimd.tensor_tensor(gathered[:, slot, here], raw[:, here], mask[:, slot, here], ALU.mult).then_inc(gather_ready, 1)

            def bond_low(s, slot, firsts=None):
                if not near:
                    pool.wait_ge(first_ready, firsts)
                    wait(pool, gather_ready, s * SUPER_GROUPS)
                pool.wait_ge(bond_high, s + 1)
                low = bond[64:128, slot, :]
                nc.gpsimd.tensor_tensor(low, bond_whole[64:128, slot, :], low, ALU.subtract).then_inc(bond_split, 1)

            def finish(s, slot, firsts):
                bond_low(s, slot, firsts)
                pool.wait_ge(bond_split, s + 1)
                clear_half(s, slot)

            def body(s, slot):
                first_pick(s, slot)
                if not first_use(s):
                    finish(s - 1, 1 - slot, s + 1)

            if near:
                paired_loop(pool, SUPERS, bond_low)
            else:
                paired_loop(pool, SUPERS, body)
                finish(SUPERS - 1, 1, SUPERS)

        def near_or_far(engine, part):
            if layer == 0:
                flag = engine.value_load(is_near[0:1, 0:1], min_val=0, max_val=1)
                with engine.If(flag > 0):
                    part(engine, True)
                with engine.Else():
                    part(engine, False)
            else:
                part(engine, False)

        with ctx, nc.Block() as block:
            @block.sync
            def _(sp):
                near_or_far(sp, sync_part)

            @block.gpsimd
            def _(pool):
                if layer == 0:
                    nc.gpsimd.memset(bond_whole[:, :, :], 0.0).then_inc(bond_cleared, 1)
                else:
                    nc.gpsimd.memset(bond[:, :, :].bitcast(F32), 0.0).then_inc(bond_cleared, 1)
                    nc.gpsimd.memset(hidden[:, :, :], 0.0).then_inc(hidden_cleared, 1)
                if layer == 0:
                    near_or_far(pool, pool_part)

            @block.vector
            def _(dve):
                near_or_far(dve, vector_part)

            @block.scalar
            def _(act):
                if layer == 1:
                    act.wait_ge(hidden_cleared, 1)
                    nc.scalar.activation(less_id[:, :], node_id[:, :], ACT.Copy, scale=-1.0).then_inc(id_ready, 1)
                    act.wait_ge(id_ready, 1)
                near_or_far(act, scalar_part)

            @block.tensor
            def _(pe):
                near_or_far(pe, tensor_part)

    def normalize(dve, step, layer, value, square, stat, root, variance_done, root_done):
        v = nc.vector
        wide = lambda a: a.unsqueeze(2).to_broadcast([128, NODE_TILES, D])
        step(v.tensor_reduce(stat[:, :], value[:, :, :], AX.X, ALU.add))
        step(v.tensor_scalar(stat[:, :], stat[:, :], 1.0 / D, None, ALU.mult))
        step(v.tensor_tensor(value[:, :, :], value[:, :, :], wide(stat[:, :]), ALU.subtract))
        step(v.tensor_tensor(square[:, :, :], value[:, :, :], value[:, :, :], ALU.mult))
        step(v.tensor_reduce(stat[:, :], square[:, :, :], AX.X, ALU.add))
        step(v.tensor_scalar(stat[:, :], stat[:, :], 1.0 / D, EPS, ALU.mult, ALU.add))
        v.sem_inc(variance_done, 1)
        dve.wait_ge(root_done, 1)
        step(v.reciprocal(root[:, :], root[:, :]))
        step(v.tensor_tensor(node_feats[:, 0:NODE_TILES, :], value[:, :, :], wide(root[:, :]), ALU.mult))

    def source_stage():
        ctx = ExitStack()
        RING = 4
        BATCH = 8
        BATCHES = TILES // BATCH
        SETS = QUARTERS // 2
        sums_ps = pb(ctx, "src_sums_ps", [128, SETS, 2 * BANK])
        node_ps = pb(ctx, "src_node_ps", [128, 2, BANK])
        place_used = sem("src_place_used")
        place_ready = sem("src_place_ready")
        high_done = sem("src_high_done")
        low_done = sem("src_low_done")
        masked_done = sem("src_masked_done")

        inner = ExitStack()
        parts = sb(inner, "src_parts", [EDGE_TILE, 2, BATCH, SPLIT * D], F32R)
        masked = sb(inner, "src_masked", [EDGE_TILE, 2, BATCH, QUARTERS, SPLIT * D], F32R)
        place = sb(inner, "src_place", [EDGE_TILE, RING, QUARTER_NODES], F32R)
        quarter_mask = sb(inner, "src_quarter_mask", [EDGE_TILE, TILES, QUARTERS], BF16)
        quarters_known = sem("src_quarters_known")
        with inner, nc.Block() as block:
            @block.scalar
            def _(act):
                def body(s, slot):
                    wait(act, masked_done, s - 1)
                    nc.scalar.activation(parts[:, slot, :, 0:D], messages[:, bass.ds(s * BATCH, BATCH), :], ACT.Copy).then_inc(high_done, 1)
                paired_loop(act, BATCHES, body)

            @block.gpsimd
            def _(pool):
                def body(s, slot):
                    if first_use(s):
                        pool.wait_ge(quarters_known, QUARTERS)
                    """Each edge's parts once for each quarter, cleared but for the quarter of its src."""
                    pool.wait_ge(high_done, s + 1)
                    nc.gpsimd.tensor_tensor(parts[:, slot, :, D:2 * D], messages[:, bass.ds(s * BATCH, BATCH), :], parts[:, slot, :, 0:D],
                                            ALU.subtract).then_inc(low_done, 1)
                    pool.wait_ge(low_done, s + 1)
                    wait(pool, place_used, s * BATCH - BATCH)
                    shape = [EDGE_TILE, BATCH, QUARTERS, SPLIT * D]
                    nc.gpsimd.tensor_tensor(masked[:, slot, :, :, :], parts[:, slot, :, :].unsqueeze(2).to_broadcast(shape),
                                            quarter_mask[:, bass.ds(s * BATCH, BATCH), :].unsqueeze(3).to_broadcast(shape), ALU.mult).then_inc(masked_done, 1)
                paired_loop(pool, BATCHES, body)

            @block.vector
            def _(dve):
                for q in range(QUARTERS):
                    nc.vector.tensor_scalar(quarter_mask[:, :, q], src_quarter[:, :], float(q), None, ALU.is_equal).then_inc(quarters_known, 1)

                def body(s, slot):
                    for t in range(BATCH):
                        wait(dve, place_used, s * BATCH + t + 1 - RING)
                        nc.vector.tensor_scalar(place[:, t % RING, :], node_iota[:, 0:QUARTER_NODES], src_quarter_col[:, bass.ds(s * BATCH + t, 1)],
                                                None, ALU.is_equal).then_inc(place_ready, 1)
                paired_loop(dve, BATCHES, body)

            @block.tensor
            def _(pe):
                spans = [(b, min(b + BANK, QUARTER_NODES)) for b in range(0, QUARTER_NODES, BANK)]
                for a in range(SETS):
                    for lo, hi in spans:
                        nc.tensor.matmul(sums_ps[:, a, lo:hi], zeros[0:EDGE_TILE, 0:128], zeros[0:EDGE_TILE, 0:hi - lo],
                                         start=True, stop=False, skip_group_check=True)

                def body(s, slot):
                    pe.wait_ge(masked_done, s + 1)
                    for t in range(BATCH):
                        pe.wait_ge(place_ready, s * BATCH + t + 1)
                        for a in range(SETS):
                            for lo, hi in spans:
                                last = nc.tensor.matmul(sums_ps[:, a, lo:hi], masked[:, slot, t, 2 * a:2 * a + 2, :].rearrange("p q c -> p (q c)"),
                                                        place[:, t % RING, lo:hi], start=False, stop=False, skip_group_check=True)
                        last.then_inc(place_used, 1)
                paired_loop(pe, BATCHES, body)

        BANK_TILES = BANK // D

        def pieces(h):
            for size in (NODE_TILE, NODE_TILE // QUARTERS):
                cut = [((h * NODE_TILE + at) // QUARTER_NODES, at, size) for at in range(0, NODE_TILE, size)]
                if all(h * NODE_TILE + at + n <= (q + 1) * QUARTER_NODES for q, at, n in cut):
                    return cut

        sums = sb(ctx, "src_sums", [128, SETS, QUARTER_NODES], F32)
        value = sb(ctx, "src_value", [128, NODE_TILES, D], F32)
        square = sb(ctx, "src_square", [128, NODE_TILES, D], F32)
        stat = sb(ctx, "src_stat", [128, NODE_TILES], F32)
        root = sb(ctx, "src_root", [128, NODE_TILES], F32)
        sums_copied = sem("src_sums_copied")
        nodes_summed = sem("src_nodes_summed")
        variance_done = sem("src_variance_done")
        root_done = sem("src_root_done")
        node_step = sem("src_node_step")
        with ctx, nc.Block() as block:
            @block.scalar
            def _(act):
                nc.scalar.activation(sums[:, 0, :], sums_ps[:, 0, 0:QUARTER_NODES], ACT.Copy).then_inc(sums_copied, 1)
                act.wait_ge(variance_done, 1)
                nc.scalar.activation(root[:, :], stat[:, :], ACT.Sqrt).then_inc(root_done, 1)

            @block.tensor
            def _(pe):
                pe.wait_ge(sums_copied, 2)
                for b in range(2):
                    for h in range(b * BANK_TILES, min((b + 1) * BANK_TILES, NODE_TILES)):
                        for q, at, n in pieces(h):
                            last = nc.tensor.matmul(node_ps[at:at + n, b, (h % BANK_TILES) * D:(h % BANK_TILES + 1) * D],
                                                    sums[:, q // 2, h * NODE_TILE + at - q * QUARTER_NODES:][:, 0:n],
                                                    sum_quarters_sb[:, (q % 2) * D:(q % 2 + 1) * D], start=True, stop=True)
                    last.then_inc(nodes_summed, 1)

            @block.vector
            def _(dve):
                v = nc.vector
                done = [0]

                def step(instruction):
                    done[0] += 1
                    instruction.then_inc(node_step, 1)
                    dve.wait_ge(node_step, done[0])

                v.tensor_copy(sums[:, 1, :], sums_ps[:, 1, 0:QUARTER_NODES]).then_inc(sums_copied, 1)
                for b in range(2):
                    dve.wait_ge(nodes_summed, b + 1)
                    at = slice(b * BANK_TILES, min((b + 1) * BANK_TILES, NODE_TILES))
                    of = node_ps[:, b, 0:(at.stop - at.start) * D].rearrange("p (h d) -> p h d", d=D)
                    step(v.tensor_tensor(value[:, at, :], of, node_feats[:, at, :], ALU.add))
                normalize(dve, step, 0, value, square, stat, root, variance_done, root_done)
                make_pairs(step, v)

    def target_stage():
        ctx = ExitStack()
        name = lambda n: f"dst_{n}"
        RING = 5
        BATCH = 40
        BATCH_GROUPS = BATCH // GROUP_TILES
        BATCHES = TILES // BATCH
        sums_ps = pb(ctx, name("sums_ps"), [COLS, ACC_BANKS * BANK])

        parts_free = sem(name("parts_free"))
        high_done = sem(name("high_done"))
        rest_done = sem(name("rest_done"))
        middle_done = sem(name("middle_done"))
        parts_ready = sem(name("parts_ready"))
        place_ready = sem(name("place_ready"))
        iota_ready = sem(name("iota_ready"))
        ones_set = sem(name("ones_set"))
        sums_done = sem(name("sums_done"))

        inner = ExitStack()
        parts = sb(inner, name("parts"), [EDGE_TILE, 2, BATCH, COLS], BF16)
        rest = sb(inner, name("rest"), [EDGE_TILE, 2, BATCH, D], F32)
        place = sb(inner, name("place"), [EDGE_TILE, RING, NODES], BF16)

        near_place = place[:, 0:2, 0:BATCH * WINDOW_NODES].rearrange("p a (t n) -> p a t n", n=WINDOW_NODES)
        window_iota = sb(inner, name("window_iota"), [EDGE_TILE, WINDOW_NODES], F32)

        def vector_part(dve, near):
            def low_parts(s, slot):
                dve.wait_ge(middle_done, s + 1)
                nc.vector.tensor_tensor(parts[:, slot, :, 2 * D:3 * D], rest[:, slot, :, :], parts[:, slot, :, D:2 * D],
                                        ALU.subtract).then_inc(parts_ready, 1)

            def body_near(s, slot):
                wait(dve, parts_free, s * BATCH - BATCH)
                shape = [EDGE_TILE, BATCH, WINDOW_NODES]
                nc.vector.tensor_tensor(near_place[:, slot, :, :], window_iota[:, :].unsqueeze(1).to_broadcast(shape),
                                        dst_near_col[:, bass.ds(s * BATCH, BATCH)].unsqueeze(2).to_broadcast(shape), ALU.is_equal).then_inc(place_ready, 1)
                low_parts(s, slot)

            def body_far(s, slot):
                low_parts(s, slot)
                for t in range(BATCH):
                    q = s * BATCH + t
                    wait(dve, parts_free, q + 1 - RING)
                    nc.vector.tensor_scalar(place[:, t % RING, :], node_iota[:, :], dst_col[:, bass.ds(q, 1)], None, ALU.is_equal).then_inc(place_ready, 1)

            if near:
                nc.vector.tensor_copy(window_iota[:, :], node_iota[:, 0:WINDOW_NODES]).then_inc(iota_ready, 1)
                dve.wait_ge(iota_ready, 1)
            paired_loop(dve, BATCHES, body_near if near else body_far)

        def tensor_part(pe, near):
            for b in range(ACC_BANKS):
                nc.tensor.matmul(sums_ps[:, b * BANK:(b + 1) * BANK], zeros[0:EDGE_TILE, 0:COLS], zeros[0:EDGE_TILE, :],
                                 start=True, stop=False, skip_group_check=True)
            pe.wait_ge(ones_set, 1)

            def body(s, slot):
                if near:
                    _, column = nc.values_load_multi_w_load_instructions(
                        first[0:1, 0, bass.ds(s * BATCH_GROUPS, BATCH_GROUPS)], engines=[mybir.EngineType.PE], min_val=0,
                        max_val=ACC_BANKS * BANK - WINDOW_NODES,
                        skip_runtime_bounds_check_because="a dst is below N, and a bank begins every SPAN nodes")
                    pe.wait_ge(place_ready, s + 1)
                pe.wait_ge(parts_ready, s + 1)
                for t in range(BATCH):
                    if near:
                        at = [(bass.ds(column[t // GROUP_TILES], WINDOW_NODES), near_place[:, slot, t, :])]
                    else:
                        pe.wait_ge(place_ready, s * BATCH + t + 1)
                        at = [(slice(b * BANK, b * BANK + min(SPAN, N - b * SPAN)), place[:, t % RING, b * SPAN:min((b + 1) * SPAN, N)])
                              for b in range(ACC_BANKS)]
                    for to, of in at:
                        last = nc.tensor.matmul(sums_ps[:, to], parts[:, slot, t, :], of, start=False, stop=False, skip_group_check=True)
                    last.then_inc(parts_free, 1)
            paired_loop(pe, BATCHES, body)

        def near_or_far(engine, part):
            flag = engine.value_load(is_near[0:1, 0:1], min_val=0, max_val=1)
            with engine.If(flag > 0):
                part(engine, True)
            with engine.Else():
                part(engine, False)

        with inner, nc.Block() as block:
            @block.gpsimd
            def _(pool):
                nc.gpsimd.memset(parts[:, :, :, COLS - 1:COLS], 1.0).then_inc(ones_set, 1)

                def body(s, slot):
                    pool.wait_ge(high_done, s + 1)
                    wait(pool, parts_ready, s - 1)
                    nc.gpsimd.tensor_tensor(rest[:, slot, :, :], messages[:, bass.ds(s * BATCH, BATCH), :], parts[:, slot, :, 0:D],
                                            ALU.subtract).then_inc(rest_done, 1)
                paired_loop(pool, BATCHES, body)

            @block.scalar
            def _(act):
                def body(s, slot):
                    wait(act, parts_free, s * BATCH - BATCH)
                    nc.scalar.activation(parts[:, slot, :, 0:D], messages[:, bass.ds(s * BATCH, BATCH), :], ACT.Copy).then_inc(high_done, 1)
                    act.wait_ge(rest_done, s + 1)
                    nc.scalar.activation(parts[:, slot, :, D:2 * D], rest[:, slot, :, :], ACT.Copy).then_inc(middle_done, 1)
                paired_loop(act, BATCHES, body)

            @block.vector
            def _(dve):
                near_or_far(dve, vector_part)

            @block.tensor
            def _(pe):
                near_or_far(pe, tensor_part)

        sums = sb(ctx, name("sums"), [COLS, NODES], F32)
        value = sb(ctx, name("value"), [128, NODE_TILES, D], F32)
        square = sb(ctx, name("square"), [128, NODE_TILES, D], F32)
        stat = sb(ctx, name("stat"), [128, NODE_TILES], F32)
        count = sb(ctx, name("count"), [128, NODE_TILES], F32)
        root = sb(ctx, name("root"), [128, NODE_TILES], F32)
        sums_copied = sem(name("sums_copied"))
        nodes_summed = sem(name("nodes_summed"))
        variance_done = sem(name("variance_done"))
        root_done = sem(name("root_done"))
        node_step = sem(name("node_step"))
        stored = sem(name("stored"))
        HALF = -(-NODE_TILES // 2)
        node_ps = pb(ctx, name("node_ps"), [128, BANK])

        def node_sums(half):
            n = HALF if half == 0 else NODE_TILES - HALF
            return node_ps[:, 0:n * (D + 1)].rearrange("p (h c) -> p h c", c=D + 1), n

        with ctx, nc.Block() as block:
            @block.scalar
            def _(act):
                for b in range(0, ACC_BANKS, 2):
                    n = SPAN if b < ACC_BANKS - 1 else NODES - b * SPAN
                    nc.scalar.activation(sums[:, b * SPAN:b * SPAN + n], sums_ps[:, b * BANK:b * BANK + n], ACT.Copy).then_inc(sums_copied, 1)
                act.wait_ge(variance_done, 1)
                nc.scalar.activation(root[:, :], stat[:, :], ACT.Sqrt).then_inc(root_done, 1)

            @block.tensor
            def _(pe):
                pe.wait_ge(node_step, 1)
                for half in range(2):
                    to, n = node_sums(half)
                    if half:
                        pe.wait_ge(node_step, 2)
                    for h in range(n):
                        tile = half * HALF + h
                        last = nc.tensor.matmul(to[:, h, :], sums[:, tile * NODE_TILE:(tile + 1) * NODE_TILE], sum_parts_sb[:, :], start=True, stop=True)
                    last.then_inc(nodes_summed, 1)

            @block.vector
            def _(dve):
                v = nc.vector
                done = [0]

                def step(instruction):
                    done[0] += 1
                    instruction.then_inc(node_step, 1)
                    dve.wait_ge(node_step, done[0])

                for b in range(1, ACC_BANKS, 2):
                    n = SPAN if b < ACC_BANKS - 1 else NODES - b * SPAN
                    v.tensor_copy(sums[:, b * SPAN:b * SPAN + n], sums_ps[:, b * BANK:b * BANK + n]).then_inc(sums_copied, 1)
                dve.wait_ge(sums_copied, ACC_BANKS)
                start = sums[:, SPAN:ACC_BANKS * SPAN].rearrange("c (b n) -> c b n", n=SPAN)[:, :, 0:WINDOW_NODES]
                step(v.tensor_tensor(start, start, sums_ps[:, 0:(ACC_BANKS - 1) * BANK].rearrange("c (b n) -> c b n", n=BANK)[:, :, SPAN:BANK], ALU.add))
                wide = lambda a: a.unsqueeze(2).to_broadcast([128, NODE_TILES, D])
                for half in range(2):
                    of, n = node_sums(half)
                    at = slice(half * HALF, half * HALF + n)
                    dve.wait_ge(nodes_summed, half + 1)
                    v.tensor_scalar(count[:, at], of[:, :, D], 1.0, None, ALU.max)
                    step(v.tensor_copy(value[:, at, :], of[:, :, 0:D]))
                step(v.reciprocal(count[:, :], count[:, :]))
                step(v.tensor_tensor(value[:, :, :], value[:, :, :], wide(count[:, :]), ALU.mult))
                step(v.tensor_tensor(value[:, :, :], value[:, :, :], b2_sb[:, :].unsqueeze(1).to_broadcast([128, NODE_TILES, D]), ALU.add))
                step(v.tensor_scalar(value[:, :, :], value[:, :, :], 0.0, None, ALU.max))
                step(v.tensor_tensor(value[:, :, :], value[:, :, :], node_feats[:, 0:NODE_TILES, :], ALU.add))
                normalize(dve, step, 1, value, square, stat, root, variance_done, root_done)
                v.sem_inc(sums_done, 1)

            @block.sync
            def _(sp):
                sp.wait_ge(sums_done, 1)
                sp.dma_start(out[0:FULL * NODE_TILE, :].rearrange("(h p) d -> p h d", p=NODE_TILE), node_feats[:, 0:FULL, :]).then_inc(stored, 16)
                sp.dma_start(out[FULL * NODE_TILE:N, :], node_feats[0:TAIL, FULL, :]).then_inc(stored, 16)
                sp.wait_ge(stored, 32)

    message_stage(0)
    source_stage()
    message_stage(1)
    target_stage()
    top.close()


def laid_out(x, src, dst, edge_attr_16, L0_gnn_kernel, L0_gnn_bias, L1_gnn_W1, L1_gnn_b1, L1_gnn_W2, L1_gnn_b2):
    a = {k: np.asarray(v) for k, v in locals().items()}
    x, src, dst, bond = a["x"], a["src"], a["dst"], a["edge_attr_16"]
    D, E, BOND = x.shape[1], src.shape[0], bond.shape[1]
    nodes = -(-x.shape[0] // NODE_TILE) * NODE_TILE
    row = np.arange(BOND * D) // D
    spread_bond = (np.arange(BOND)[:, None] == row[None, :]).reshape(BOND, -1, 128)
    spread_x = np.arange(128)[:, None] % D == np.arange(128)[None, :] % D
    column = np.arange(128)
    sum_quarters = (column // (SPLIT * D) * D + column % D)[:, None] == np.arange(2 * D)[None, :]
    sum_parts = np.zeros((PARTS * D + 1, D + 1), np.float32)
    sum_parts[np.arange(PARTS * D), np.arange(PARTS * D) % D] = 1
    sum_parts[PARTS * D, D] = 1
    laid = dict(
        x=x, src_rows=src, dst_rows=dst, src_cols=src.reshape(-1, EDGE_TILE).T, dst_cols=dst.reshape(-1, EDGE_TILE).T,
        bond_rows=bond.T,
        edge_kernel=a["L0_gnn_kernel"].reshape(BOND, D, D).transpose(0, 2, 1).reshape(-1, 128, D).transpose(1, 0, 2),
        edge_bias=a["L0_gnn_bias"].reshape(D, D).T,
        w1_node=a["L1_gnn_W1"].T[:D], w1_edge=a["L1_gnn_W1"].T[D:], b1=a["L1_gnn_b1"][:, None],
        w2=a["L1_gnn_W2"].T, b2=a["L1_gnn_b2"][None, :],
        node_row=np.arange(nodes, dtype=np.int16)[None, :],
        node_col=np.arange(-(-nodes // (HALVES * NODE_TILE)) * NODE_TILE, dtype=np.float32).reshape(-1, NODE_TILE).T,
        window_col=(np.arange(128) // SPLIT).astype(np.float32)[:, None],
        span_starts=np.arange(SPAN, nodes - WINDOW_NODES, SPAN, dtype=np.float32)[None, :],
        spread_bond=spread_bond.astype(np.float32), spread_x=spread_x.astype(np.float32),
        sum_quarters=sum_quarters.astype(np.float32), sum_parts=sum_parts, identity=np.eye(128, dtype=np.float32))
    return {k: np.ascontiguousarray(v) for k, v in laid.items()}


def kernel(**inputs):
    import concourse.bacc as bacc
    from concourse.bass_utils import run_bass_kernel_spmd

    arrays = laid_out(**inputs)
    nc = bacc.Bacc("TRN2", target_bir_lowering=False, num_devices=1)
    args = {n: nc.dram_tensor(n, v.shape, mybir.dt.from_np(v.dtype), kind="ExternalInput").ap() for n, v in arrays.items()}
    out = nc.dram_tensor("out", arrays["x"].shape, F32, kind="ExternalOutput").ap()
    gnn_program(nc, **args, out=out)
    r = run_bass_kernel_spmd(nc, [arrays], core_ids=[0])
    return r.results[0]["out"]
```
